# Optimizing a Trainium2 kernel written in Bass

```python
import numpy as np
import jax
import jax.numpy as jnp

def _softmax(x, axis=-1):
    return jax.nn.softmax(x, axis=axis)

def _gelu(x):
    return jax.nn.gelu(x, approximate=True)

def _silu(x):
    return jax.nn.silu(x)

def _sigmoid(x):
    return jax.nn.sigmoid(x)

def _layernorm(x, axis=-1, eps=1e-05):
    m = jnp.mean(x, axis=axis, keepdims=True)
    v = jnp.var(x, axis=axis, keepdims=True)
    return (x - m) / jnp.sqrt(v + eps)

def _scatter_add(tgt, idx, src, axis=0):
    return tgt.at[idx].add(src)

def _segment_sum(src, seg, n):
    return jax.ops.segment_sum(src, seg, n)
kernel_name = 'mk_adj_seq_d1_adj_r2_011d78'

def setup_inputs(seed: int=0):
    np.random.seed(seed)
    _w = jnp.asarray

    def _rec_inputs():
        import jax
        import jax.numpy as jnp
        _gk = jax.random.key(seed)
        x = -0.0005207 + 1.001 * jax.random.normal(jax.random.fold_in(_gk, 1), (8192, 128), jnp.float32)
        _a = jax.random.bernoulli(jax.random.fold_in(_gk, 2), 0.000488281, (8192, 8192))
        _a = jnp.logical_or(_a, jnp.swapaxes(_a, -1, -2))
        _a = jnp.logical_or(_a, jnp.eye(8192, dtype=bool))
        adj = _a.astype(jnp.int32)
        return (x, adj)
    x, adj = _rec_inputs()

    def _L0_gnn_setup():
        import jax, jax.numpy as jnp
        import numpy as np
        B, D = (4096, 128)
        EPS = 1e-05
        NEG_SLOPE = 0.2
        FILL_VAL = -1000000000.0

        def _layer_norm(x, gamma, beta):
            mu = jnp.mean(x, axis=-1, keepdims=True)
            var = jnp.mean(jnp.square(x - mu), axis=-1, keepdims=True)
            return (x - mu) * jax.lax.rsqrt(var + EPS) * gamma + beta
        key = jax.random.key(seed)
        ks = jax.random.split(key, 8)
        h = jax.random.normal(ks[0], (B, D), dtype=jnp.float32)
        adj = jax.random.randint(ks[1], (B, B), 0, 2, dtype=jnp.int32)
        W_w = jax.random.normal(ks[2], (D, D), dtype=jnp.float32) / np.sqrt(D)
        a1 = jax.random.normal(ks[3], (D,), dtype=jnp.float32) / np.sqrt(2 * D)
        a2 = jax.random.normal(ks[4], (D,), dtype=jnp.float32) / np.sqrt(2 * D)
        gamma = 1.0 + 0.02 * jax.random.normal(ks[5], (D,), dtype=jnp.float32)
        beta = 0.02 * jax.random.normal(ks[6], (D,), dtype=jnp.float32)
        return {'h': h, 'adj': adj, 'W_w': W_w, 'a1': a1, 'a2': a2, 'gamma': gamma, 'beta': beta}
    _L0_gnn_all = _L0_gnn_setup()
    _L0_gnn_in = {k: v for k, v in _L0_gnn_all.items() if k in ('W_w', 'a1', 'a2', 'gamma', 'beta')}
    del _L0_gnn_all
    return {'x': x, 'adj': adj, 'L0_gnn_W_w': _L0_gnn_in['W_w'], 'L0_gnn_a1': _L0_gnn_in['a1'], 'L0_gnn_a2': _L0_gnn_in['a2'], 'L0_gnn_gamma': _L0_gnn_in['gamma'], 'L0_gnn_beta': _L0_gnn_in['beta']}

def reference(x, adj, L0_gnn_W_w, L0_gnn_a1, L0_gnn_a2, L0_gnn_gamma, L0_gnn_beta):
    import jax
    import jax.numpy as jnp

    def _L0_gnn_ref(h, adj, W_w, a1, a2, gamma, beta):
        import jax, jax.numpy as jnp
        import numpy as np
        B, D = (4096, 128)
        EPS = 1e-05
        NEG_SLOPE = 0.2
        FILL_VAL = -1000000000.0

        def _layer_norm(x, gamma, beta):
            mu = jnp.mean(x, axis=-1, keepdims=True)
            var = jnp.mean(jnp.square(x - mu), axis=-1, keepdims=True)
            return (x - mu) * jax.lax.rsqrt(var + EPS) * gamma + beta
        Wh = h @ W_w.T
        si = Wh @ a1
        sj = Wh @ a2
        e = si[:, None] + sj[None, :]
        e = jnp.where(e >= 0, e, NEG_SLOPE * e)
        mask = adj == 0
        e_masked = jnp.where(mask, FILL_VAL, e)
        alpha = jax.nn.softmax(e_masked, axis=1)
        all_masked = jnp.all(mask, axis=1, keepdims=True)
        alpha = jnp.where(all_masked, 0.0, alpha)
        agg = alpha @ Wh
        elu = jnp.where(agg > 0, agg, jnp.expm1(agg))
        return _layer_norm(h + elu, gamma, beta)
    x = _L0_gnn_ref(x, adj, L0_gnn_W_w, L0_gnn_a1, L0_gnn_a2, L0_gnn_gamma, L0_gnn_beta)
    return x

_drawn_inputs = setup_inputs


def setup_inputs(seed=0):
    import zlib

    import numpy as np

    out = dict(_drawn_inputs(seed))
    spreads = {}
    factors = {}
    for name, (base, spread) in spreads.items():
        noise = np.random.default_rng([zlib.crc32(name.encode()), seed]).standard_normal(out[name].shape)
        drawn = base * np.exp(spread * noise) if base else spread * noise
        out[name] = jnp.asarray(drawn.astype(out[name].dtype))
    for name, factor in factors.items():
        out[name] = (out[name] * factor).astype(out[name].dtype)
    return out
```

```python
from contextlib import ExitStack

import concourse.bass as bass
from concourse import mybir

F32 = mybir.dt.float32
F32R = mybir.dt.float32r
BF16 = mybir.dt.bfloat16
I32 = mybir.dt.int32
U32 = mybir.dt.uint32
ALU = mybir.AluOpType
ACT = mybir.ActivationFunctionType
AX_X = mybir.AxisListType.X
RMAX = bass.bass_isa.ReduceOp.max

P = 128
N = 8192
D = 128
NB = N // P
SLOPE = 0.2
EPS = 1e-5
TINY = 1e-37

GB = 8
GI = GB * P
NG = N // GI
CB = 4
CJ = CB * P
BUFS = 4
CHUNKS = NB // CB
BODY = CB * BUFS
BODIES = NB // BODY
SLOTS = 4
LOOK = CB
DC = D + 2
PER_BANK = 3
BANKS = (GB + PER_BANK - 1) // PER_BANK
SPLIT = 384
PIECE = NB // 4


def gat_kernel(nc, x, adj, w, a1, a2, gamma, beta, out):
    ctx = ExitStack()
    with ctx:
        def sb(name, shape, dt=F32):
            return ctx.enter_context(nc.sbuf_tensor(name, shape, dt))

        def sem(name):
            return ctx.enter_context(nc.semaphore(name))

        adj_sb = sb("adj_sb", [P, BUFS, GB * CJ], I32)
        table = sb("table", [P, NB, DC + D], F32R)
        p_rows = sb("p_rows", [P, 2, GI])
        wgt = sb("wgt", [P, SLOTS, GI])
        wgt_h = sb("wgt_h", [P, SLOTS, GI], F32R)
        wgt_l = sb("wgt_l", [P, SLOTS, GI], F32R)
        sums = sb("sums", [P, GB, DC])
        agg = sb("agg", [P, GB, D])
        work = sb("work", [P, GB, D])
        x_res = sb("x_res", [P, GB, D])
        ident = sb("ident", [P, P])
        zeros = sb("zeros", [P, P], BF16)
        w_sb = sb("w_sb", [P, D])
        a_sb = sb("a_sb", [P, 2])
        wt = sb("wt", [P, DC])
        gamma_sb = sb("gamma_sb", [P, D])
        beta_sb = sb("beta_sb", [P, D])
        s_cols = sb("s_cols", [P, NB, 2])
        top = sb("top", [P, 2])
        gap = sb("gap", [P, NB])
        rise = sb("rise", [P, NB])
        q_cols = sb("q_cols", [P, NB])
        g_cols = sb("g_cols", [P, NB])
        p_cols = sb("p_cols", [P, NB])
        p_t = sb("p_t", [NB, P])
        den = sb("den", [P, GB])
        rden = sb("rden", [P, GB])
        stats = sb("stats", [P, GB, 6])
        mean_sum = sb("mean_sum", [P, GB])
        mean_gap = sb("mean_gap", [P, GB])
        sq_sum = sb("sq_sum", [P, GB])
        var_eps = sb("var_eps", [P, GB])
        neg_mean = sb("neg_mean", [P, GB])
        rstd = sb("rstd", [P, GB])
        shift = sb("shift", [P, GB])
        minus_half = sb("minus_half", [P, GB])

        at_ps = [ctx.enter_context(nc.psum_tensor(f"at_ps{k}", [P, GI], F32)) for k in range(2)]
        acc = ctx.enter_context(nc.psum_tensor("acc", [P, BANKS, 512], F32))
        misc = ctx.enter_context(nc.psum_tensor("misc", [P, 512], F32))
        p_dram = nc.dram_tensor("p_dram", [NB, P], F32, kind="Internal").ap()

        x_st = [wgt[:, u, :].rearrange("p (b k) -> p b k", b=GB) for u in range(2)]
        xt_sb = [wgt[:, 2 + u, :] for u in range(2)]
        wh = adj_sb[:, 2:4, :].bitcast(F32).rearrange("p a (b k) -> p (a b) k", k=D)
        qh_all, ql_all = table[:, :, 0:D], table[:, :, DC:DC + D]

        w_loaded = sem("w_loaded")
        affine_loaded = sem("affine_loaded")
        x_loaded = [sem(f"x_loaded{u}") for u in range(2)]
        x_turned = sem("x_turned")
        xt_ready = sem("xt_ready")
        wh_ps = sem("wh_ps")
        wh_ready = sem("wh_ready")
        ident_zero = sem("ident_zero")
        consts_ready = sem("consts_ready")
        wt_ps = sem("wt_ps")
        wt_ready = sem("wt_ready")
        top_part = sem("top_part")
        top_ready = sem("top_ready")
        gap_ready = sem("gap_ready")
        factors_ready = sem("factors_ready")
        p_turned = sem("p_turned")
        p_t_ready = sem("p_t_ready")
        p_stored = sem("p_stored")
        p_loaded = sem("p_loaded")
        scaled = sem("scaled")
        qh_ready = sem("qh_ready")
        table_dve = sem("table_dve")
        table_pool = sem("table_pool")
        adj_loaded = [sem(f"adj_loaded{k}") for k in range(BUFS)]
        at_ready = sem("at_ready")
        e_ready = sem("e_ready")
        eh_ready = sem("eh_ready")
        el_dve = sem("el_dve")
        el_pool = sem("el_pool")
        used = sem("used")
        group_done = sem("group_done")
        acc_free = sem("acc_free")
        den_ready = sem("den_ready")
        rden_ready = sem("rden_ready")
        agg_ready = sem("agg_ready")
        neg_ready = sem("neg_ready")
        elu_ready = sem("elu_ready")
        elu_sum = sem("elu_sum")
        x_res_loaded = sem("x_res_loaded")
        y_ready = sem("y_ready")
        stats_ready = sem("stats_ready")
        pair_ready = sem("pair_ready")
        moment_ready = sem("moment_ready")
        var_ready = sem("var_ready")
        rstd_ready = sem("rstd_ready")
        shift_ready = sem("shift_ready")
        norm_ready = sem("norm_ready")
        gamma_done = sem("gamma_done")
        out_ready = sem("out_ready")
        out_stored = sem("out_stored")

        def acc_of(b):
            c = (b % PER_BANK) * DC
            return acc[:, b // PER_BANK, c:c + DC]

        def blocks_in(bank):
            return min(PER_BANK, GB - bank * PER_BANK)

        def rows_of(t, g):
            return t[bass.ds(g * GI, GI), :].rearrange("(b p) k -> p b k", p=P)

        block = ctx.enter_context(nc.Block())

        @block.sync
        def _(sp):
            def load_chunk(g, c, buf):
                src = adj[bass.ds(g * GI, GI), bass.ds(c * CJ, CJ)].rearrange("(b p) j -> p b j", p=P)
                sp.dma_start(adj_sb[:, buf, :].rearrange("p (b j) -> p b j", b=GB), src).then_inc(adj_loaded[buf], 16)

            def load_quad(g, quad):
                for k in range(BUFS):
                    sp.wait_ge(at_ready, g * NB + (quad * BUFS + k - BUFS + 1) * CB)
                    load_chunk(g, quad * BUFS + k, k)

            def load_p(g):
                row = p_dram[bass.ds(g * GB, GB), :].rearrange("(o b) p -> o (b p)", o=1)
                sp.dma_start(p_rows[:, bass.ds(g % 2, 1), :],
                             row.broadcast_to([P, GI])).then_inc(p_loaded, 16)

            def load_x(g):
                sp.wait_ge(y_ready, g)
                sp.dma_start(x_res[:, :, :], rows_of(x, g)).then_inc(x_res_loaded, 16)

            def store(g):
                sp.wait_ge(out_ready, g + 1)
                sp.dma_start(rows_of(out, g), work[:, :, :]).then_inc(out_stored, 16)

            sp.dma_start(w_sb[:, :], w).then_inc(w_loaded, 16)
            sp.dma_start(a_sb[:, 0:1], a1.rearrange("(k o) -> k o", o=1)).then_inc(w_loaded, 16)
            sp.dma_start(a_sb[:, 1:2], a2.rearrange("(k o) -> k o", o=1)).then_inc(w_loaded, 16)
            for u in range(2):
                sp.dma_start(x_st[u], rows_of(x, u)).then_inc(x_loaded[u], 16)
            with sp.Fori(1, NG // 2) as n:
                for u in range(2):
                    sp.wait_ge(x_turned, n * 2 + (u - 1))
                    sp.dma_start(x_st[u], rows_of(x, n * 2 + u)).then_inc(x_loaded[u], 16)
            sp.dma_start(gamma_sb[:, :], gamma.partition_broadcast(P)).then_inc(affine_loaded, 16)
            sp.dma_start(beta_sb[:, :], beta.partition_broadcast(P)).then_inc(affine_loaded, 16)
            load_chunk(0, 0, 0)
            load_chunk(0, 1, 1)
            sp.wait_ge(p_t_ready, 1)
            sp.dma_start(p_dram, p_t[:, :]).then_inc(p_stored, 16)
            sp.wait_ge(p_stored, 16)
            load_p(0)
            sp.wait_ge(table_dve, 3)
            sp.wait_ge(table_pool, 2)
            load_chunk(0, 2, 2)
            load_chunk(0, 3, 3)

            load_quad(0, 1)
            load_quad(0, 2)
            load_p(1)
            load_x(0)
            load_quad(0, 3)
            load_quad(1, 0)
            with sp.Fori(1, NG - 1) as g:
                load_quad(g, 1)
                load_quad(g, 2)
                sp.wait_ge(e_ready, g * NB)
                load_p(g + 1)
                load_x(g)
                store(g - 1)
                load_quad(g, 3)
                load_quad(g + 1, 0)
            load_quad(NG - 1, 1)
            load_quad(NG - 1, 2)
            load_x(NG - 1)
            store(NG - 2)
            load_quad(NG - 1, 3)
            store(NG - 1)
            sp.wait_ge(out_stored, 16 * NG + 16)

        @block.tensor
        def _(pe):
            def turn_tiles(buf, k, half):
                for b in range(GB):
                    src = adj_sb[:, buf, b * CJ + k * P:b * CJ + (k + 1) * P].bitcast(F32)
                    mm = nc.tensor.transpose(at_ps[half][:, b * P:(b + 1) * P], src, ident[:, :])
                return mm

            def multiply(step, j, slot):
                hi = table[:, bass.ds(j, 1), 0:DC].rearrange("p o k -> p (o k)")
                lo = table[:, bass.ds(j, 1), DC:DC + D].rearrange("p o k -> p (o k)")
                pe.wait_ge(eh_ready, step + 1)
                for b in range(GB):
                    e = wgt_h[:, slot, b * P:(b + 1) * P]
                    nc.tensor.matmul(acc_of(b), e, hi, start=False, stop=False, skip_group_check=True)
                    nc.tensor.matmul(acc_of(b)[:, 0:D], e, lo, start=False, stop=False, skip_group_check=True)
                pe.wait_ge(el_dve, step + (SLOTS + 1))
                pe.wait_ge(el_pool, step + (SLOTS + 1))
                for b in range(GB):
                    mm = nc.tensor.matmul(acc_of(b), wgt_l[:, slot, b * P:(b + 1) * P], hi,
                                          start=False, stop=False, skip_group_check=True)
                mm.then_inc(used, 1)

            def turn_ahead(g, body, s):
                a = s + LOOK
                buf, k = (a // CB) % BUFS, a % CB
                if k == 0:
                    pe.wait_ge(adj_loaded[buf], (g * BODIES + body) * 16 + (1 + a // BODY) * 16)
                pe.wait_ge(e_ready, g * NB + body * BODY + (a - 1))
                turn_tiles(buf, k, a % 2).then_inc(at_ready, 1)

            def open_group(g):
                for r in range(BANKS):
                    pe.wait_ge(acc_free, g * BANKS + (r + 1))
                    nc.tensor.matmul(acc[:, r, 0:2], zeros[:, :], zeros[:, 0:2], start=True, stop=False,
                                     skip_group_check=True)

            def close_group():
                for r in range(BANKS):
                    mm = nc.tensor.matmul(acc[:, r, 0:2], zeros[:, :], zeros[:, 0:2], start=False, stop=True,
                                          skip_group_check=True)
                mm.then_inc(group_done, 1)

            def body_steps(g, body, ahead=BODY):
                for s in range(BODY):
                    multiply(g * NB + body * BODY + s, body * BODY + s, s % SLOTS)
                    if s < ahead:
                        turn_ahead(g, body, s)

            pe.wait_ge(consts_ready, 3)
            pe.wait_ge(w_loaded, 16 * 3)
            nc.tensor.transpose(misc[:, 0:D], w_sb[:, :], ident[:, :])
            nc.tensor.matmul(misc[:, D:DC], w_sb[:, :], a_sb[:, :], start=True, stop=True).then_inc(wt_ps, 1)
            pe.wait_ge(wt_ready, 1)

            def turn_x(m, u, pair, first):
                pe.wait_ge(x_loaded[u], pair * 16 + 16)
                if not first:
                    pe.wait_ge(xt_ready, m - 1)
                for b in range(GB):
                    mm = nc.tensor.transpose(at_ps[u][:, b * P:(b + 1) * P], x_st[u][:, b, :], ident[:, :])
                mm.then_inc(x_turned, 1)

            def project(m, u, first):
                pe.wait_ge(xt_ready, m + 1)
                if not first:
                    pe.wait_ge(wh_ready, m)
                for b in range(GB):
                    mm = nc.tensor.matmul(acc_of(b), xt_sb[u][:, b * P:(b + 1) * P], wt[:, :], start=True, stop=True)
                mm.then_inc(wh_ps, 1)

            turn_x(0, 0, 0, True)
            turn_x(1, 1, 0, True)
            project(0, 0, True)
            project(1, 1, False)
            with pe.Fori(1, NG // 2) as n:
                turn_x(n * 2, 0, n, False)
                turn_x(n * 2 + 1, 1, n, False)
                project(n * 2, 0, False)
                project(n * 2 + 1, 1, False)

            pe.wait_ge(factors_ready, 3)
            nc.tensor.transpose(misc[0:NB, 0:P], p_cols[:, :], ident[:, :]).then_inc(p_turned, 1)

            pe.wait_ge(adj_loaded[0], 16)
            for k in range(CB):
                if k < 2:
                    pe.wait_ge(xt_ready, NG)
                else:
                    pe.wait_ge(e_ready, k - 1)
                turn_tiles(0, k, k % 2).then_inc(at_ready, 1)
            pe.wait_ge(table_dve, 3)
            pe.wait_ge(table_pool, 2)
            pe.wait_ge(wh_ready, NG)
            with pe.Fori(0, NG - 1) as g:
                open_group(g)
                with pe.Fori(0, BODIES) as body:
                    body_steps(g, body)
                close_group()
            open_group(NG - 1)
            with pe.Fori(0, BODIES - 1) as body:
                body_steps(NG - 1, body)
            body_steps(NG - 1, BODIES - 1, BODY - LOOK)
            close_group()

        @block.scalar
        def _(act):
            def high_part(step, slot):
                act.wait_ge(e_ready, step + 1)
                act.wait_ge(used, step + 1)
                nc.scalar.copy(wgt_h[:, slot, :], wgt[:, slot, :]).then_inc(eh_ready, 1)

            def take_sums(g):
                act.wait_ge(group_done, g + 1)
                for r in range(BANKS):
                    k = blocks_in(r)
                    nc.scalar.copy(sums[:, r * PER_BANK:r * PER_BANK + k, :].rearrange("p b k -> p (b k)"),
                                   acc[:, r, 0:k * DC]).then_inc(acc_free, 1)

            def divide(g, lo, hi):
                act.wait_ge(rden_ready, g + 1)
                for b in range(lo, hi):
                    nc.scalar.activation(agg[:, b, :], sums[:, b, 0:D], ACT.Copy,
                                         scale=rden[:, b:b + 1]).then_inc(agg_ready, 1)

            def negative(g):
                act.wait_ge(agg_ready, g * GB + GB)
                act.wait_ge(out_stored, g * 16 + 16)
                nc.scalar.activation(work[:, :, :], agg[:, :, :], ACT.Relu, scale=-1.0).then_inc(neg_ready, 1)

            def exponential(g):
                act.wait_ge(neg_ready, g + 1)
                nc.scalar.activation(work[:, :, :], work[:, :, :], ACT.Exp, scale=-1.0).then_inc(elu_ready, 1)

            def positive(g):
                nc.scalar.activation(agg[:, :, :], agg[:, :, :], ACT.Relu).then_inc(elu_ready, 1)

            def normalise(g, lo, hi):
                act.wait_ge(shift_ready, g + 1)
                for b in range(lo, hi):
                    nc.scalar.activation(work[:, b, :], agg[:, b, :], ACT.Identity, scale=rstd[:, b:b + 1],
                                         bias=shift[:, b:b + 1]).then_inc(norm_ready, 1)

            half = GB // 2
            finals = {2: [take_sums], 4: [lambda g: divide(g, 0, half)], 5: [lambda g: divide(g, half, GB)],
                      6: [negative], 7: [exponential], 8: [positive],
                      13: [lambda g: normalise(g, 0, half)], 14: [lambda g: normalise(g, half, GB)]}

            act.wait_ge(wt_ps, 1)
            nc.scalar.copy(wt[:, :], misc[:, 0:DC]).then_inc(wt_ready, 1)

            def copy_xt(m, u, first):
                act.wait_ge(x_turned, m + 1)
                if not first:
                    act.wait_ge(wh_ps, m - 1)
                nc.scalar.copy(xt_sb[u], at_ps[u][:, :]).then_inc(xt_ready, 1)

            copy_xt(0, 0, True)
            copy_xt(1, 1, True)
            with act.Fori(1, NG // 2) as n:
                for u in range(2):
                    copy_xt(n * 2 + u, u, False)

            act.wait_ge(gap_ready, 2)
            nc.scalar.activation(p_cols[:, :], rise[:, :], ACT.Exp, scale=SLOPE - 1.0).then_inc(factors_ready, 1)
            nc.scalar.activation(q_cols[:, :], gap[:, :], ACT.Exp, scale=SLOPE).then_inc(factors_ready, 1)
            nc.scalar.activation(g_cols[:, :], gap[:, :], ACT.Exp, scale=1.0 - SLOPE).then_inc(factors_ready, 1)
            act.wait_ge(factors_ready, 2)
            nc.scalar.copy(table[:, :, D:D + 1], q_cols[:, :].rearrange("p (b o) -> p b o", o=1)).then_inc(qh_ready, 1)
            act.wait_ge(p_turned, 1)
            nc.scalar.copy(p_t[:, :], misc[0:NB, 0:P]).then_inc(p_t_ready, 1)
            for n in range(NB // PIECE):
                act.wait_ge(scaled, n + 1)
                nc.scalar.copy(qh_all[:, n * PIECE:(n + 1) * PIECE, :],
                               wh[:, n * PIECE:(n + 1) * PIECE, :]).then_inc(qh_ready, 1)

            def steps(g, body, last=None):
                for s in range(BODY):
                    high_part(g * NB + body * BODY + s, s % SLOTS)
                    if last is not None:
                        for final in finals.get(s, []):
                            final(last)

            with act.Fori(0, BODIES) as body:
                steps(0, body)
            with act.Fori(1, NG) as g:
                steps(g, 0, g - 1)
                with act.Fori(1, BODIES) as body:
                    steps(g, body)
            for s in sorted(finals):
                for final in finals[s]:
                    final(NG - 1)

        @block.vector
        def _(dve):
            def weights(g, step, j, slot, half):
                dve.wait_ge(at_ready, step + 1)
                dve.wait_ge(el_dve, step + 1)
                dve.wait_ge(el_pool, step + 1)
                nc.vector.scalar_tensor_tensor(
                    out=wgt[:, slot, :], in0=p_rows[:, bass.ds(g % 2, 1), :].rearrange("p o i -> p (o i)"),
                    scalar=g_cols[:, bass.ds(j, 1)], in1=at_ps[half][:, :].bitcast(U32),
                    op0=ALU.max, op1=ALU.min).then_inc(e_ready, 1)

            def low_part(step, slot):
                dve.wait_ge(eh_ready, step + 1)
                nc.vector.tensor_tensor(wgt_l[:, slot, 0:SPLIT], wgt[:, slot, 0:SPLIT],
                                        wgt_h[:, slot, 0:SPLIT].bitcast(F32), ALU.subtract).then_inc(el_dve, 1)

            def invert(g):
                dve.wait_ge(acc_free, g * BANKS + 2 * BANKS)
                nc.vector.scalar_tensor_tensor(out=den[:, :], in0=sums[:, :, D:D + 1].rearrange("p b o -> p (b o)"),
                                               scalar=TINY, in1=sums[:, :, D + 1:DC].rearrange("p b o -> p (b o)"),
                                               op0=ALU.max, op1=ALU.add).then_inc(den_ready, 1)
                dve.wait_ge(den_ready, g + 1)
                nc.vector.reciprocal(rden[:, :], den[:, :]).then_inc(rden_ready, 1)

            def join_elu(g):
                dve.wait_ge(elu_ready, g * 2 + 2)
                nc.vector.scalar_tensor_tensor(out=agg[:, :, :], in0=work[:, :, :], scalar=-1.0, in1=agg[:, :, :],
                                               op0=ALU.add, op1=ALU.add).then_inc(elu_sum, 1)

            def residual(g):
                dve.wait_ge(elu_sum, g + 1)
                dve.wait_ge(x_res_loaded, g * 16 + 16)
                nc.vector.tensor_tensor(agg[:, :, :], agg[:, :, :], x_res[:, :, :], ALU.add).then_inc(y_ready, 1)

            def statistics(g, lo, hi):
                dve.wait_ge(y_ready, g + 1)
                for b in range(lo, hi):
                    nc.vector.bn_stats(stats[:, b, :], agg[:, b, :]).then_inc(stats_ready, 1)

            def moments(g):
                def stat(k):
                    return stats[:, :, k:k + 1].rearrange("p b o -> p (b o)")

                dve.wait_ge(stats_ready, g * GB + GB)
                nc.vector.tensor_tensor(mean_sum[:, :], stat(1), stat(4), ALU.add).then_inc(pair_ready, 1)
                nc.vector.tensor_tensor(mean_gap[:, :], stat(1), stat(4), ALU.subtract).then_inc(pair_ready, 1)
                nc.vector.tensor_tensor(sq_sum[:, :], stat(2), stat(5), ALU.add).then_inc(pair_ready, 1)
                dve.wait_ge(pair_ready, g * 3 + 3)
                nc.vector.tensor_scalar(neg_mean[:, :], mean_sum[:, :], -0.5, None, ALU.mult).then_inc(moment_ready, 1)
                nc.vector.tensor_scalar(sq_sum[:, :], sq_sum[:, :], 1.0 / D, EPS, ALU.mult,
                                        ALU.add).then_inc(moment_ready, 1)
                nc.vector.tensor_tensor(mean_gap[:, :], mean_gap[:, :], mean_gap[:, :],
                                        ALU.mult).then_inc(moment_ready, 1)
                dve.wait_ge(moment_ready, g * 3 + 3)
                nc.vector.scalar_tensor_tensor(out=var_eps[:, :], in0=mean_gap[:, :], scalar=0.25, in1=sq_sum[:, :],
                                               op0=ALU.mult, op1=ALU.add).then_inc(var_ready, 1)

            half = GB // 2
            finals = {3: [invert], 8: [join_elu], 9: [residual], 10: [lambda g: statistics(g, 0, half)],
                      11: [lambda g: statistics(g, half, GB)], 12: [moments]}

            def take_wh(m):
                dve.wait_ge(wh_ps, m + 1)
                for r in range(BANKS):
                    k = blocks_in(r)
                    src = acc[:, r, 0:k * DC].rearrange("p (b k) -> p b k", k=DC)
                    nc.vector.tensor_copy(wh[:, bass.ds(m * GB + r * PER_BANK, k), :], src[:, :, 0:D])
                    last = nc.vector.tensor_copy(s_cols[:, bass.ds(m * GB + r * PER_BANK, k), :], src[:, :, D:DC])
                last.then_inc(wh_ready, 1)

            with dve.Fori(0, NG) as m:
                take_wh(m)

            dve.wait_ge(wh_ready, NG)
            s_j = s_cols[:, :, 1:2].rearrange("p b o -> p (b o)")
            s_i = s_cols[:, :, 0:1].rearrange("p b o -> p (b o)")
            nc.vector.reduce_max(top[:, 0:1], s_j, AX_X).then_inc(top_part, 1)
            dve.wait_ge(top_ready, 1)
            nc.vector.tensor_scalar(rise[:, :], s_i, top[:, 1:2], 0.0, ALU.add, ALU.max).then_inc(gap_ready, 1)
            nc.vector.tensor_scalar(gap[:, :], s_j, top[:, 1:2], None, ALU.subtract).then_inc(gap_ready, 1)

            dve.wait_ge(factors_ready, 2)
            for n in range(NB // PIECE):
                lo, hi = n * PIECE, (n + 1) * PIECE
                q_wide = q_cols[:, lo:hi].rearrange("p (b o) -> p b o", o=1).broadcast_to([P, PIECE, D])
                nc.vector.tensor_tensor(wh[:, lo:hi, :], wh[:, lo:hi, :], q_wide, ALU.mult).then_inc(scaled, 1)
            dve.wait_ge(qh_ready, 1)
            nc.vector.tensor_tensor(table[:, :, D + 1:DC], q_cols[:, :].rearrange("p (b o) -> p b o", o=1),
                                    table[:, :, D:D + 1].bitcast(F32), ALU.subtract).then_inc(table_dve, 1)
            for n in range(2):
                dve.wait_ge(qh_ready, n + 2)
                nc.vector.tensor_tensor(ql_all[:, n * PIECE:(n + 1) * PIECE, :], wh[:, n * PIECE:(n + 1) * PIECE, :],
                                        qh_all[:, n * PIECE:(n + 1) * PIECE, :].bitcast(F32),
                                        ALU.subtract).then_inc(table_dve, 1)

            def steps(g, body, first=0, last=None):
                for s in range(first, BODY):
                    step = g * NB + body * BODY + s
                    if s == 0 and last is not None:
                        dve.wait_ge(p_loaded, g * 16 + 16)
                    weights(g, step, body * BODY + s, s % SLOTS, s % 2)
                    low_part(step - 1, (s - 1) % SLOTS)
                    if last is not None:
                        for final in finals.get(s, []):
                            final(last)

            dve.wait_ge(factors_ready, 3)
            dve.wait_ge(p_loaded, 16)
            weights(0, 0, 0, 0, 0)
            steps(0, 0, first=1)
            with dve.Fori(1, BODIES) as body:
                steps(0, body)
            with dve.Fori(1, NG) as g:
                steps(g, 0, last=g - 1)
                with dve.Fori(1, BODIES) as body:
                    steps(g, body)
            low_part(NG * NB - 1, (NG * NB - 1) % SLOTS)
            for s in sorted(finals):
                for final in finals[s]:
                    final(NG - 1)

        @block.gpsimd
        def _(pool):
            def low_part(step, slot):
                pool.wait_ge(eh_ready, step + 1)
                nc.gpsimd.tensor_tensor(wgt_l[:, slot, SPLIT:GI], wgt[:, slot, SPLIT:GI],
                                        wgt_h[:, slot, SPLIT:GI].bitcast(F32), ALU.subtract).then_inc(el_pool, 1)

            def deviation(g):
                pool.wait_ge(var_ready, g + 1)
                nc.gpsimd.tensor_tensor(rstd[:, :], var_eps[:, :], minus_half[:, :], ALU.pow).then_inc(rstd_ready, 1)
                pool.wait_ge(rstd_ready, g + 1)
                nc.gpsimd.tensor_tensor(shift[:, :], neg_mean[:, :], rstd[:, :], ALU.mult).then_inc(shift_ready, 1)

            def times_gamma(g):
                pool.wait_ge(norm_ready, g * GB + GB)
                wide = gamma_sb[:, :].rearrange("p (o k) -> p o k", o=1).broadcast_to([P, GB, D])
                nc.gpsimd.tensor_tensor(work[:, :, :], work[:, :, :], wide, ALU.mult).then_inc(gamma_done, 1)

            def plus_beta(g):
                pool.wait_ge(gamma_done, g + 1)
                wide = beta_sb[:, :].rearrange("p (o k) -> p o k", o=1).broadcast_to([P, GB, D])
                nc.gpsimd.tensor_tensor(work[:, :, :], work[:, :, :], wide, ALU.add).then_inc(out_ready, 1)

            finals = {12: [deviation], 14: [times_gamma], 15: [plus_beta]}

            nc.gpsimd.memset(ident[:, :], 0.0).then_inc(ident_zero, 1)
            pool.wait_ge(ident_zero, 1)
            nc.gpsimd.affine_select(out=ident[:, :], in_=ident[:, :], compare_op=ALU.not_equal, fill=1.0, base=0,
                                    pattern=[[-1, P]], channel_multiplier=1).then_inc(consts_ready, 1)
            nc.gpsimd.memset(zeros[:, :], 0.0).then_inc(consts_ready, 1)
            nc.gpsimd.memset(minus_half[:, :], -0.5).then_inc(consts_ready, 1)
            pool.sem_inc(el_dve, SLOTS)
            pool.sem_inc(el_pool, SLOTS)
            pool.sem_inc(used, SLOTS)
            pool.sem_inc(acc_free, BANKS)
            pool.sem_inc(out_stored, 16)
            pool.wait_ge(top_part, 1)
            nc.gpsimd.partition_all_reduce(top[:, 1:2], top[:, 0:1], P, RMAX).then_inc(top_ready, 1)
            for n in range(2, 4):
                pool.wait_ge(qh_ready, n + 2)
                nc.gpsimd.tensor_tensor(ql_all[:, n * PIECE:(n + 1) * PIECE, :], wh[:, n * PIECE:(n + 1) * PIECE, :],
                                        qh_all[:, n * PIECE:(n + 1) * PIECE, :].bitcast(F32),
                                        ALU.subtract).then_inc(table_pool, 1)

            def steps(g, body, last=None):
                for s in range(BODY):
                    low_part(g * NB + body * BODY + s, s % SLOTS)
                    if last is not None:
                        for final in finals.get(s, []):
                            final(last)

            pool.wait_ge(affine_loaded, 16 * 2)
            with pool.Fori(0, BODIES) as body:
                steps(0, body)
            with pool.Fori(1, NG) as g:
                steps(g, 0, last=g - 1)
                with pool.Fori(1, BODIES) as body:
                    steps(g, body)
            for s in sorted(finals):
                for final in finals[s]:
                    final(NG - 1)


_INS = ["x", "adj", "L0_gnn_W_w", "L0_gnn_a1", "L0_gnn_a2", "L0_gnn_gamma", "L0_gnn_beta"]
_OUT = ((N, D), "float32")


def kernel(**inputs):
    import numpy as _np
    import concourse.bacc as _bacc
    from concourse import mybir as _mybir
    from concourse.bass_utils import run_bass_kernel_spmd as _run

    nc = _bacc.Bacc("TRN2", target_bir_lowering=False, num_devices=1)
    arrays, args = {}, []
    for name in _INS:
        a = _np.ascontiguousarray(inputs[name])
        arrays[f"in_{name}"] = a
        args.append(nc.dram_tensor(f"in_{name}", a.shape, _mybir.dt.from_np(a.dtype), kind="ExternalInput").ap())
    shape, dtype = _OUT
    out = nc.dram_tensor("out", shape, _mybir.dt.from_np(_np.dtype(dtype)), kind="ExternalOutput").ap()
    gat_kernel(nc, *args, out)
    return _run(nc, [arrays], core_ids=[0]).results[0]["out"]
```

```python
from contextlib import ExitStack

import concourse.bass as bass
from concourse import mybir

F32 = mybir.dt.float32
F32R = mybir.dt.float32r
BF16 = mybir.dt.bfloat16
I32 = mybir.dt.int32
U16 = mybir.dt.uint16
ALU = mybir.AluOpType
ACT = mybir.ActivationFunctionType
AX_X = mybir.AxisListType.X
RMAX = bass.bass_isa.ReduceOp.max

P = 128
N = 8192
D = 128
NB = N // P
SLOPE = 0.2
EPS = 1e-5
TINY = 1e-37

GB = 4
GI = GB * P
NG = N // GI
PAIR = 2
STEPS = NB // PAIR
CS = 4
CJ = CS * PAIR * P
BUFS = 4
BODY = CS * BUFS
BODIES = STEPS // BODY
SLOTS = 4
LOOK = SLOTS
DC = D + 2
TW = DC + D
CONV = 1
SPLIT = 256
XB = 8
XG = NB // XB
PER_BANK = 3
BANKS = (XB + PER_BANK - 1) // PER_BANK
PIECE = NB // 4


def gat_kernel(nc, x, adj, w, a1, a2, gamma, beta, out):
    ctx = ExitStack()
    with ctx:
        def sb(name, shape, dt=F32):
            return ctx.enter_context(nc.sbuf_tensor(name, shape, dt))

        def sem(name):
            return ctx.enter_context(nc.semaphore(name))

        adj_sb = sb("adj_sb", [P, BUFS, GB * CJ], I32)
        adj_bf = sb("adj_bf", [P, SLOTS, GB, PAIR * P], BF16)
        table = sb("table", [P, NB, TW], F32R)
        p_rows = sb("p_rows", [P, 2, GI])
        wgt = sb("wgt", [P, SLOTS, PAIR * GI])
        wgt_h = sb("wgt_h", [P, SLOTS, PAIR * GI], F32R)
        wgt_l = sb("wgt_l", [P, SLOTS, PAIR * GI], F32R)
        sums = sb("sums", [P, GB, TW])
        agg = sb("agg", [P, GB, D])
        work = sb("work", [P, GB, D])
        x_res = sb("x_res", [P, GB, D])
        ident = sb("ident", [P, P])
        ident_bf = sb("ident_bf", [P, P], BF16)
        zeros = sb("zeros", [P, P], BF16)
        w_sb = sb("w_sb", [P, D])
        a_sb = sb("a_sb", [P, 2])
        wt = sb("wt", [P, DC])
        gamma_sb = sb("gamma_sb", [P, D])
        beta_sb = sb("beta_sb", [P, D])
        s_cols = sb("s_cols", [P, NB, 2])
        top = sb("top", [P, 2])
        gap = sb("gap", [P, NB])
        rise = sb("rise", [P, NB])
        q_cols = sb("q_cols", [P, NB])
        g_cols = sb("g_cols", [P, NB])
        p_cols = sb("p_cols", [P, NB])
        p_t = sb("p_t", [NB, P])
        den = sb("den", [P, GB])
        rden = sb("rden", [P, GB])
        stats = sb("stats", [P, GB, 6])
        mean_sum = sb("mean_sum", [P, GB])
        mean_gap = sb("mean_gap", [P, GB])
        sq_sum = sb("sq_sum", [P, GB])
        var_eps = sb("var_eps", [P, GB])
        neg_mean = sb("neg_mean", [P, GB])
        rstd = sb("rstd", [P, GB])
        shift = sb("shift", [P, GB])
        minus_half = sb("minus_half", [P, GB])

        at_ps = ctx.enter_context(nc.psum_tensor("at_ps", [P, SLOTS, 512], F32))
        acc = ctx.enter_context(nc.psum_tensor("acc", [P, GB, 512], F32))
        p_dram = nc.dram_tensor("p_dram", [NB, P], F32, kind="Internal").ap()

        x_st = [wgt[:, u, :].rearrange("p (b k) -> p b k", b=XB) for u in range(2)]
        xt_sb = [wgt[:, 2 + u, :] for u in range(2)]
        xt_ps = [at_ps[:, 2 * u:2 * u + 2, :].rearrange("p a k -> p (a k)") for u in range(2)]
        misc = acc[:, BANKS, :]
        wh = adj_sb[:, 2:4, :].bitcast(F32).rearrange("p a (b k) -> p (a b) k", k=D)
        qh_all, ql_all = table[:, :, 0:D], table[:, :, DC:DC + D]

        w_loaded = sem("w_loaded")
        affine_loaded = sem("affine_loaded")
        x_loaded = [sem(f"x_loaded{u}") for u in range(2)]
        x_turned = sem("x_turned")
        xt_ready = sem("xt_ready")
        wh_ps = sem("wh_ps")
        wh_ready = sem("wh_ready")
        ident_zero = sem("ident_zero")
        consts_ready = sem("consts_ready")
        wt_ps = sem("wt_ps")
        wt_ready = sem("wt_ready")
        top_part = sem("top_part")
        top_ready = sem("top_ready")
        gap_ready = sem("gap_ready")
        factors_ready = sem("factors_ready")
        p_turned = sem("p_turned")
        p_t_ready = sem("p_t_ready")
        p_stored = sem("p_stored")
        p_loaded = sem("p_loaded")
        scaled = sem("scaled")
        qh_ready = sem("qh_ready")
        table_dve = sem("table_dve")
        table_pool = sem("table_pool")
        adj_loaded = [sem(f"adj_loaded{k}") for k in range(BUFS)]
        conv_act = sem("conv_act")
        conv_dve = sem("conv_dve")
        at_ready = sem("at_ready")
        e_ready = sem("e_ready")
        eh_ready = sem("eh_ready")
        el_dve = sem("el_dve")
        el_pool = sem("el_pool")
        used = sem("used")
        group_done = sem("group_done")
        acc_free = sem("acc_free")
        numer_ready = sem("numer_ready")
        den_ready = sem("den_ready")
        rden_ready = sem("rden_ready")
        agg_ready = sem("agg_ready")
        neg_ready = sem("neg_ready")
        elu_ready = sem("elu_ready")
        elu_sum = sem("elu_sum")
        x_res_loaded = sem("x_res_loaded")
        y_ready = sem("y_ready")
        stats_ready = sem("stats_ready")
        pair_ready = sem("pair_ready")
        moment_ready = sem("moment_ready")
        var_ready = sem("var_ready")
        rstd_ready = sem("rstd_ready")
        shift_ready = sem("shift_ready")
        norm_ready = sem("norm_ready")
        gamma_done = sem("gamma_done")
        out_ready = sem("out_ready")
        out_stored = sem("out_stored")

        def xacc_of(b):
            c = (b % PER_BANK) * DC
            return acc[:, b // PER_BANK, c:c + DC]

        def blocks_in(bank):
            return min(PER_BANK, XB - bank * PER_BANK)

        def rows_of(t, first, blocks):
            return t[bass.ds(first * P, blocks * P), :].rearrange("(b p) k -> p b k", p=P)

        def ahead_of(s):
            a = s + LOOK
            return (a // CS) % BUFS, a % CS, a // BODY

        def columns(t, buf, k, lo, hi):
            c = k * PAIR * P
            return t[:, buf, :].rearrange("p (b j) -> p b j", b=GB)[:, lo:hi, c:c + PAIR * P]

        block = ctx.enter_context(nc.Block())

        @block.sync
        def _(sp):
            def load_chunk(g, c, buf):
                src = adj[bass.ds(g * GI, GI), bass.ds(c * CJ, CJ)].rearrange("(b p) j -> p b j", p=P)
                sp.dma_start(adj_sb[:, buf, :].rearrange("p (b j) -> p b j", b=GB), src).then_inc(adj_loaded[buf], 16)

            def load_quad(g, quad):
                for k in range(BUFS):
                    sp.wait_ge(conv_act, g * STEPS + (quad * BUFS + k - BUFS + 1) * CS)
                    sp.wait_ge(conv_dve, g * STEPS + (quad * BUFS + k - BUFS + 1) * CS)
                    load_chunk(g, quad * BUFS + k, k)

            def load_p(g):
                row = p_dram[bass.ds(g * GB, GB), :].rearrange("(o b) p -> o (b p)", o=1)
                sp.dma_start(p_rows[:, bass.ds(g % 2, 1), :],
                             row.broadcast_to([P, GI])).then_inc(p_loaded, 16)

            def load_x(g):
                sp.wait_ge(y_ready, g)
                sp.dma_start(x_res[:, :, :], rows_of(x, g * GB, GB)).then_inc(x_res_loaded, 16)

            def store(g):
                sp.wait_ge(out_ready, g + 1)
                sp.dma_start(rows_of(out, g * GB, GB), work[:, :, :]).then_inc(out_stored, 16)

            sp.dma_start(w_sb[:, :], w).then_inc(w_loaded, 16)
            sp.dma_start(a_sb[:, 0:1], a1.rearrange("(k o) -> k o", o=1)).then_inc(w_loaded, 16)
            sp.dma_start(a_sb[:, 1:2], a2.rearrange("(k o) -> k o", o=1)).then_inc(w_loaded, 16)
            for u in range(2):
                sp.dma_start(x_st[u], rows_of(x, u * XB, XB)).then_inc(x_loaded[u], 16)
            with sp.Fori(1, XG // 2) as n:
                for u in range(2):
                    sp.wait_ge(x_turned, n * 2 + (u - 1))
                    sp.dma_start(x_st[u], rows_of(x, (n * 2 + u) * XB, XB)).then_inc(x_loaded[u], 16)
            sp.dma_start(gamma_sb[:, :], gamma.partition_broadcast(P)).then_inc(affine_loaded, 16)
            sp.dma_start(beta_sb[:, :], beta.partition_broadcast(P)).then_inc(affine_loaded, 16)
            load_chunk(0, 0, 0)
            load_chunk(0, 1, 1)
            sp.wait_ge(p_t_ready, 1)
            sp.dma_start(p_dram, p_t[:, :]).then_inc(p_stored, 16)
            sp.wait_ge(p_stored, 16)
            load_p(0)
            sp.wait_ge(table_dve, 3)
            sp.wait_ge(table_pool, 2)
            load_chunk(0, 2, 2)
            load_chunk(0, 3, 3)

            load_quad(0, 1)
            load_p(1)
            load_x(0)
            load_quad(1, 0)
            with sp.Fori(1, NG - 1) as g:
                load_quad(g, 1)
                sp.wait_ge(e_ready, g * STEPS)
                load_p(g + 1)
                load_x(g)
                store(g - 1)
                load_quad(g + 1, 0)
            load_quad(NG - 1, 1)
            load_x(NG - 1)
            store(NG - 2)
            store(NG - 1)
            sp.wait_ge(out_stored, 16 * NG + 16)

        @block.tensor
        def _(pe):
            def turn_tiles(slot):
                tile = at_ps[:, slot, :].bitcast(BF16)
                for k in range(PAIR):
                    for b in range(GB):
                        c = (k * GB + b) * P
                        mm = nc.tensor.transpose(tile[:, c:c + P], adj_bf[:, slot, b, k * P:(k + 1) * P], ident_bf[:, :])
                mm.then_inc(at_ready, 1)

            def multiply(step, j, slot):
                pe.wait_ge(eh_ready, step + 1)
                for k in range(PAIR):
                    row = table[:, bass.ds(j + k, 1), :].rearrange("p o k -> p (o k)")
                    for b in range(GB):
                        c = k * GI + b * P
                        nc.tensor.matmul(acc[:, b, 0:TW], wgt_h[:, slot, c:c + P], row,
                                         start=False, stop=False, skip_group_check=True)
                pe.wait_ge(el_dve, step + (SLOTS + 1))
                pe.wait_ge(el_pool, step + (SLOTS + 1))
                for k in range(PAIR):
                    high = table[:, bass.ds(j + k, 1), 0:DC].rearrange("p o k -> p (o k)")
                    for b in range(GB):
                        c = k * GI + b * P
                        mm = nc.tensor.matmul(acc[:, b, 0:DC], wgt_l[:, slot, c:c + P], high,
                                              start=False, stop=False, skip_group_check=True)
                mm.then_inc(used, 1)

            def turn_ahead(step, slot):
                pe.wait_ge(conv_act, step + (LOOK + 1))
                pe.wait_ge(conv_dve, step + (LOOK + 1))
                pe.wait_ge(e_ready, step + (LOOK - SLOTS + 1))
                turn_tiles(slot)

            def open_group(g):
                for b in range(GB):
                    pe.wait_ge(acc_free, g * GB + (b + 1))
                    nc.tensor.matmul(acc[:, b, 0:2], zeros[:, :], zeros[:, 0:2], start=True, stop=False,
                                     skip_group_check=True)

            def close_group():
                for b in range(GB):
                    mm = nc.tensor.matmul(acc[:, b, 0:2], zeros[:, :], zeros[:, 0:2], start=False, stop=True,
                                          skip_group_check=True)
                mm.then_inc(group_done, 1)

            def body_steps(g, body, ahead=BODY):
                for s in range(BODY):
                    step = g * STEPS + body * BODY + s
                    multiply(step, (body * BODY + s) * PAIR, s % SLOTS)
                    if s < ahead:
                        turn_ahead(step, s % SLOTS)

            pe.wait_ge(consts_ready, 4)
            pe.wait_ge(w_loaded, 16 * 3)
            nc.tensor.transpose(misc[:, 0:D], w_sb[:, :], ident[:, :])
            nc.tensor.matmul(misc[:, D:DC], w_sb[:, :], a_sb[:, :], start=True, stop=True).then_inc(wt_ps, 1)
            pe.wait_ge(wt_ready, 1)

            def turn_x(m, u, pair, first):
                pe.wait_ge(x_loaded[u], pair * 16 + 16)
                if not first:
                    pe.wait_ge(xt_ready, m - 1)
                for b in range(XB):
                    mm = nc.tensor.transpose(xt_ps[u][:, b * P:(b + 1) * P], x_st[u][:, b, :], ident[:, :])
                mm.then_inc(x_turned, 1)

            def project(m, u, first):
                pe.wait_ge(xt_ready, m + 1)
                if not first:
                    pe.wait_ge(wh_ready, m)
                for b in range(XB):
                    mm = nc.tensor.matmul(xacc_of(b), xt_sb[u][:, b * P:(b + 1) * P], wt[:, :], start=True, stop=True)
                mm.then_inc(wh_ps, 1)

            turn_x(0, 0, 0, True)
            turn_x(1, 1, 0, True)
            project(0, 0, True)
            project(1, 1, False)
            with pe.Fori(1, XG // 2) as n:
                turn_x(n * 2, 0, n, False)
                turn_x(n * 2 + 1, 1, n, False)
                project(n * 2, 0, False)
                project(n * 2 + 1, 1, False)

            pe.wait_ge(factors_ready, 3)
            nc.tensor.transpose(misc[0:NB, 0:P], p_cols[:, :], ident[:, :]).then_inc(p_turned, 1)

            for step in range(LOOK):
                if step == 0:
                    pe.wait_ge(xt_ready, XG)
                pe.wait_ge(conv_act, step + 1)
                pe.wait_ge(conv_dve, step + 1)
                turn_tiles(step)
            pe.wait_ge(table_dve, 3)
            pe.wait_ge(table_pool, 2)
            pe.wait_ge(wh_ready, XG)
            pe.wait_ge(p_t_ready, 1)
            with pe.Fori(0, NG - 1) as g:
                open_group(g)
                with pe.Fori(0, BODIES) as body:
                    body_steps(g, body)
                close_group()
            open_group(NG - 1)
            with pe.Fori(0, BODIES - 1) as body:
                body_steps(NG - 1, body)
            body_steps(NG - 1, BODIES - 1, BODY - LOOK)
            close_group()

        @block.scalar
        def _(act):
            def convert(step, buf, k, slot, first=False):
                if not first:
                    act.wait_ge(at_ready, step - (SLOTS - 1))
                nc.scalar.copy(adj_bf[:, slot, CONV:GB, :], columns(adj_sb, buf, k, CONV, GB)).then_inc(conv_act, 1)

            def convert_ahead(g, body, s):
                buf, k, use = ahead_of(s)
                if k == 0:
                    act.wait_ge(adj_loaded[buf], (g * BODIES + body) * 16 + (1 + use) * 16)
                convert(g * STEPS + body * BODY + (s + LOOK), buf, k, s % SLOTS)

            def high_part(step, slot):
                act.wait_ge(e_ready, step + 1)
                act.wait_ge(used, step + 1)
                nc.scalar.copy(wgt_h[:, slot, :], wgt[:, slot, :]).then_inc(eh_ready, 1)

            def take_sums(g):
                act.wait_ge(group_done, g + 1)
                for b in range(GB):
                    nc.scalar.copy(sums[:, b, :], acc[:, b, 0:TW]).then_inc(acc_free, 1)

            def divide(g, lo, hi):
                act.wait_ge(rden_ready, g + 1)
                act.wait_ge(numer_ready, g + 1)
                for b in range(lo, hi):
                    nc.scalar.activation(agg[:, b, :], sums[:, b, 0:D], ACT.Copy,
                                         scale=rden[:, b:b + 1]).then_inc(agg_ready, 1)

            def negative(g):
                act.wait_ge(agg_ready, g * GB + GB)
                act.wait_ge(out_stored, g * 16 + 16)
                nc.scalar.activation(work[:, :, :], agg[:, :, :], ACT.Relu, scale=-1.0).then_inc(neg_ready, 1)

            def exponential(g):
                act.wait_ge(neg_ready, g + 1)
                nc.scalar.activation(work[:, :, :], work[:, :, :], ACT.Exp, scale=-1.0).then_inc(elu_ready, 1)

            def positive(g):
                nc.scalar.activation(agg[:, :, :], agg[:, :, :], ACT.Relu).then_inc(elu_ready, 1)

            def normalise(g, lo, hi):
                act.wait_ge(shift_ready, g + 1)
                for b in range(lo, hi):
                    nc.scalar.activation(work[:, b, :], agg[:, b, :], ACT.Identity, scale=rstd[:, b:b + 1],
                                         bias=shift[:, b:b + 1]).then_inc(norm_ready, 1)

            half = GB // 2
            finals = {2: [take_sums], 4: [lambda g: divide(g, 0, half)], 5: [lambda g: divide(g, half, GB)],
                      6: [negative], 7: [exponential], 8: [positive],
                      13: [lambda g: normalise(g, 0, half)], 14: [lambda g: normalise(g, half, GB)]}

            act.wait_ge(wt_ps, 1)
            nc.scalar.copy(wt[:, :], misc[:, 0:DC]).then_inc(wt_ready, 1)

            def copy_xt(m, u, first):
                act.wait_ge(x_turned, m + 1)
                if not first:
                    act.wait_ge(wh_ps, m - 1)
                nc.scalar.copy(xt_sb[u], xt_ps[u]).then_inc(xt_ready, 1)

            copy_xt(0, 0, True)
            copy_xt(1, 1, True)
            with act.Fori(1, XG // 2) as n:
                for u in range(2):
                    copy_xt(n * 2 + u, u, False)

            act.wait_ge(gap_ready, 2)
            nc.scalar.activation(p_cols[:, :], rise[:, :], ACT.Exp, scale=SLOPE - 1.0).then_inc(factors_ready, 1)
            nc.scalar.activation(q_cols[:, :], gap[:, :], ACT.Exp, scale=SLOPE).then_inc(factors_ready, 1)
            nc.scalar.activation(g_cols[:, :], gap[:, :], ACT.Exp, scale=1.0 - SLOPE).then_inc(factors_ready, 1)
            act.wait_ge(factors_ready, 2)
            nc.scalar.copy(table[:, :, D:D + 1], q_cols[:, :].rearrange("p (b o) -> p b o", o=1)).then_inc(qh_ready, 1)
            act.wait_ge(p_turned, 1)
            nc.scalar.copy(p_t[:, :], misc[0:NB, 0:P]).then_inc(p_t_ready, 1)
            for n in range(NB // PIECE):
                act.wait_ge(scaled, n + 1)
                nc.scalar.copy(qh_all[:, n * PIECE:(n + 1) * PIECE, :],
                               wh[:, n * PIECE:(n + 1) * PIECE, :]).then_inc(qh_ready, 1)

            def steps(g, body, last=None, ahead=BODY):
                for s in range(BODY):
                    if s < ahead:
                        convert_ahead(g, body, s)
                    high_part(g * STEPS + body * BODY + s, s % SLOTS)
                    if last is not None:
                        for final in finals.get(s, []):
                            final(last)

            act.wait_ge(adj_loaded[0], 16)
            for k in range(LOOK):
                convert(k, 0, k, k, first=True)
            with act.Fori(0, BODIES) as body:
                steps(0, body)
            with act.Fori(1, NG - 1) as g:
                steps(g, 0, g - 1)
                with act.Fori(1, BODIES) as body:
                    steps(g, body)
            steps(NG - 1, 0, NG - 2)
            steps(NG - 1, BODIES - 1, ahead=BODY - LOOK)
            for s in sorted(finals):
                for final in finals[s]:
                    final(NG - 1)

        @block.vector
        def _(dve):
            def convert(step, buf, k, slot, first=False):
                if not first:
                    dve.wait_ge(at_ready, step - (SLOTS - 1))
                nc.vector.tensor_copy(adj_bf[:, slot, 0:CONV, :], columns(adj_sb, buf, k, 0, CONV)).then_inc(conv_dve, 1)

            def convert_ahead(g, body, s):
                buf, k, use = ahead_of(s)
                if k == 0:
                    dve.wait_ge(adj_loaded[buf], (g * BODIES + body) * 16 + (1 + use) * 16)
                convert(g * STEPS + body * BODY + (s + LOOK), buf, k, s % SLOTS)

            def weights(g, step, j, slot):
                dve.wait_ge(at_ready, step + 1)
                dve.wait_ge(el_dve, step + 1)
                dve.wait_ge(el_pool, step + 1)
                for k in range(PAIR):
                    ins = nc.vector.scalar_tensor_tensor(
                        out=wgt[:, slot, k * GI:(k + 1) * GI],
                        in0=p_rows[:, bass.ds(g % 2, 1), :].rearrange("p o i -> p (o i)"),
                        scalar=g_cols[:, bass.ds(j + k, 1)],
                        in1=at_ps[:, slot, :].bitcast(U16)[:, k * GI:(k + 1) * GI],
                        op0=ALU.max, op1=ALU.min)
                ins.then_inc(e_ready, 1)

            def low_part(step, slot):
                dve.wait_ge(eh_ready, step + 1)
                nc.vector.tensor_tensor(wgt_l[:, slot, 0:SPLIT], wgt[:, slot, 0:SPLIT],
                                        wgt_h[:, slot, 0:SPLIT].bitcast(F32), ALU.subtract).then_inc(el_dve, 1)

            def invert(g):
                dve.wait_ge(acc_free, g * GB + 2 * GB)
                nc.vector.scalar_tensor_tensor(out=den[:, :], in0=sums[:, :, D:D + 1].rearrange("p b o -> p (b o)"),
                                               scalar=TINY, in1=sums[:, :, D + 1:DC].rearrange("p b o -> p (b o)"),
                                               op0=ALU.max, op1=ALU.add).then_inc(den_ready, 1)
                nc.vector.tensor_tensor(sums[:, :, 0:D], sums[:, :, 0:D], sums[:, :, DC:TW],
                                        ALU.add).then_inc(numer_ready, 1)
                dve.wait_ge(den_ready, g + 1)
                nc.vector.reciprocal(rden[:, :], den[:, :]).then_inc(rden_ready, 1)

            def join_elu(g):
                dve.wait_ge(elu_ready, g * 2 + 2)
                nc.vector.scalar_tensor_tensor(out=agg[:, :, :], in0=work[:, :, :], scalar=-1.0, in1=agg[:, :, :],
                                               op0=ALU.add, op1=ALU.add).then_inc(elu_sum, 1)

            def residual(g):
                dve.wait_ge(elu_sum, g + 1)
                dve.wait_ge(x_res_loaded, g * 16 + 16)
                nc.vector.tensor_tensor(agg[:, :, :], agg[:, :, :], x_res[:, :, :], ALU.add).then_inc(y_ready, 1)

            def statistics(g, lo, hi):
                dve.wait_ge(y_ready, g + 1)
                for b in range(lo, hi):
                    nc.vector.bn_stats(stats[:, b, :], agg[:, b, :]).then_inc(stats_ready, 1)

            def moments(g):
                def stat(k):
                    return stats[:, :, k:k + 1].rearrange("p b o -> p (b o)")

                dve.wait_ge(stats_ready, g * GB + GB)
                nc.vector.tensor_tensor(mean_sum[:, :], stat(1), stat(4), ALU.add).then_inc(pair_ready, 1)
                nc.vector.tensor_tensor(mean_gap[:, :], stat(1), stat(4), ALU.subtract).then_inc(pair_ready, 1)
                nc.vector.tensor_tensor(sq_sum[:, :], stat(2), stat(5), ALU.add).then_inc(pair_ready, 1)
                dve.wait_ge(pair_ready, g * 3 + 3)
                nc.vector.tensor_scalar(neg_mean[:, :], mean_sum[:, :], -0.5, None, ALU.mult).then_inc(moment_ready, 1)
                nc.vector.tensor_scalar(sq_sum[:, :], sq_sum[:, :], 1.0 / D, EPS, ALU.mult,
                                        ALU.add).then_inc(moment_ready, 1)
                nc.vector.tensor_tensor(mean_gap[:, :], mean_gap[:, :], mean_gap[:, :],
                                        ALU.mult).then_inc(moment_ready, 1)
                dve.wait_ge(moment_ready, g * 3 + 3)
                nc.vector.scalar_tensor_tensor(out=var_eps[:, :], in0=mean_gap[:, :], scalar=0.25, in1=sq_sum[:, :],
                                               op0=ALU.mult, op1=ALU.add).then_inc(var_ready, 1)

            half = GB // 2
            finals = {3: [invert], 8: [join_elu], 9: [residual], 10: [lambda g: statistics(g, 0, half)],
                      11: [lambda g: statistics(g, half, GB)], 12: [moments]}

            def take_wh(m):
                dve.wait_ge(wh_ps, m + 1)
                for r in range(BANKS):
                    k = blocks_in(r)
                    src = acc[:, r, 0:k * DC].rearrange("p (b k) -> p b k", k=DC)
                    nc.vector.tensor_copy(wh[:, bass.ds(m * XB + r * PER_BANK, k), :], src[:, :, 0:D])
                    last = nc.vector.tensor_copy(s_cols[:, bass.ds(m * XB + r * PER_BANK, k), :], src[:, :, D:DC])
                last.then_inc(wh_ready, 1)

            with dve.Fori(0, XG) as m:
                take_wh(m)

            dve.wait_ge(wh_ready, XG)
            s_j = s_cols[:, :, 1:2].rearrange("p b o -> p (b o)")
            s_i = s_cols[:, :, 0:1].rearrange("p b o -> p (b o)")
            nc.vector.reduce_max(top[:, 0:1], s_j, AX_X).then_inc(top_part, 1)
            dve.wait_ge(top_ready, 1)
            nc.vector.tensor_scalar(rise[:, :], s_i, top[:, 1:2], 0.0, ALU.add, ALU.max).then_inc(gap_ready, 1)
            nc.vector.tensor_scalar(gap[:, :], s_j, top[:, 1:2], None, ALU.subtract).then_inc(gap_ready, 1)

            dve.wait_ge(factors_ready, 2)
            for n in range(NB // PIECE):
                lo, hi = n * PIECE, (n + 1) * PIECE
                q_wide = q_cols[:, lo:hi].rearrange("p (b o) -> p b o", o=1).broadcast_to([P, PIECE, D])
                nc.vector.tensor_tensor(wh[:, lo:hi, :], wh[:, lo:hi, :], q_wide, ALU.mult).then_inc(scaled, 1)
            dve.wait_ge(qh_ready, 1)
            nc.vector.tensor_tensor(table[:, :, D + 1:DC], q_cols[:, :].rearrange("p (b o) -> p b o", o=1),
                                    table[:, :, D:D + 1].bitcast(F32), ALU.subtract).then_inc(table_dve, 1)
            for n in range(2):
                dve.wait_ge(qh_ready, n + 2)
                nc.vector.tensor_tensor(ql_all[:, n * PIECE:(n + 1) * PIECE, :], wh[:, n * PIECE:(n + 1) * PIECE, :],
                                        qh_all[:, n * PIECE:(n + 1) * PIECE, :].bitcast(F32),
                                        ALU.subtract).then_inc(table_dve, 1)

            def steps(g, body, first=0, last=None, ahead=BODY):
                for s in range(first, BODY):
                    step = g * STEPS + body * BODY + s
                    if s == 0 and last is not None:
                        dve.wait_ge(p_loaded, g * 16 + 16)
                    if s < ahead:
                        convert_ahead(g, body, s)
                    weights(g, step, (body * BODY + s) * PAIR, s % SLOTS)
                    low_part(step - 1, (s - 1) % SLOTS)
                    if last is not None:
                        for final in finals.get(s, []):
                            final(last)

            dve.wait_ge(adj_loaded[0], 16)
            for k in range(LOOK):
                convert(k, 0, k, k, first=True)
            dve.wait_ge(factors_ready, 3)
            dve.wait_ge(p_loaded, 16)
            convert_ahead(0, 0, 0)
            weights(0, 0, 0, 0)
            steps(0, 0, first=1)
            with dve.Fori(1, BODIES) as body:
                steps(0, body)
            with dve.Fori(1, NG - 1) as g:
                steps(g, 0, last=g - 1)
                with dve.Fori(1, BODIES) as body:
                    steps(g, body)
            steps(NG - 1, 0, last=NG - 2)
            steps(NG - 1, BODIES - 1, ahead=BODY - LOOK)
            low_part(NG * STEPS - 1, (NG * STEPS - 1) % SLOTS)
            for s in sorted(finals):
                for final in finals[s]:
                    final(NG - 1)

        @block.gpsimd
        def _(pool):
            def low_part(step, slot):
                pool.wait_ge(eh_ready, step + 1)
                nc.gpsimd.tensor_tensor(wgt_l[:, slot, SPLIT:PAIR * GI], wgt[:, slot, SPLIT:PAIR * GI],
                                        wgt_h[:, slot, SPLIT:PAIR * GI].bitcast(F32), ALU.subtract).then_inc(el_pool, 1)

            def deviation(g):
                pool.wait_ge(var_ready, g + 1)
                nc.gpsimd.tensor_tensor(rstd[:, :], var_eps[:, :], minus_half[:, :], ALU.pow).then_inc(rstd_ready, 1)
                pool.wait_ge(rstd_ready, g + 1)
                nc.gpsimd.tensor_tensor(shift[:, :], neg_mean[:, :], rstd[:, :], ALU.mult).then_inc(shift_ready, 1)

            def times_gamma(g):
                pool.wait_ge(norm_ready, g * GB + GB)
                wide = gamma_sb[:, :].rearrange("p (o k) -> p o k", o=1).broadcast_to([P, GB, D])
                nc.gpsimd.tensor_tensor(work[:, :, :], work[:, :, :], wide, ALU.mult).then_inc(gamma_done, 1)

            def plus_beta(g):
                pool.wait_ge(gamma_done, g + 1)
                wide = beta_sb[:, :].rearrange("p (o k) -> p o k", o=1).broadcast_to([P, GB, D])
                nc.gpsimd.tensor_tensor(work[:, :, :], work[:, :, :], wide, ALU.add).then_inc(out_ready, 1)

            finals = {12: [deviation], 14: [times_gamma], 15: [plus_beta]}

            nc.gpsimd.memset(ident[:, :], 0.0).then_inc(ident_zero, 1)
            pool.wait_ge(ident_zero, 1)
            nc.gpsimd.affine_select(out=ident[:, :], in_=ident[:, :], compare_op=ALU.not_equal, fill=1.0, base=0,
                                    pattern=[[-1, P]], channel_multiplier=1).then_inc(consts_ready, 1)
            pool.wait_ge(consts_ready, 1)
            nc.gpsimd.tensor_copy(ident_bf[:, :], ident[:, :]).then_inc(consts_ready, 1)
            nc.gpsimd.memset(zeros[:, :], 0.0).then_inc(consts_ready, 1)
            nc.gpsimd.memset(minus_half[:, :], -0.5).then_inc(consts_ready, 1)
            pool.sem_inc(el_dve, SLOTS)
            pool.sem_inc(el_pool, SLOTS)
            pool.sem_inc(used, SLOTS)
            pool.sem_inc(acc_free, GB)
            pool.sem_inc(out_stored, 16)
            pool.wait_ge(top_part, 1)
            nc.gpsimd.partition_all_reduce(top[:, 1:2], top[:, 0:1], P, RMAX).then_inc(top_ready, 1)
            for n in range(2, 4):
                pool.wait_ge(qh_ready, n + 2)
                nc.gpsimd.tensor_tensor(ql_all[:, n * PIECE:(n + 1) * PIECE, :], wh[:, n * PIECE:(n + 1) * PIECE, :],
                                        qh_all[:, n * PIECE:(n + 1) * PIECE, :].bitcast(F32),
                                        ALU.subtract).then_inc(table_pool, 1)

            def steps(g, body, last=None):
                for s in range(BODY):
                    low_part(g * STEPS + body * BODY + s, s % SLOTS)
                    if last is not None:
                        for final in finals.get(s, []):
                            final(last)

            pool.wait_ge(affine_loaded, 16 * 2)
            with pool.Fori(0, BODIES) as body:
                steps(0, body)
            with pool.Fori(1, NG) as g:
                steps(g, 0, last=g - 1)
                with pool.Fori(1, BODIES) as body:
                    steps(g, body)
            for s in sorted(finals):
                for final in finals[s]:
                    final(NG - 1)


_INS = ["x", "adj", "L0_gnn_W_w", "L0_gnn_a1", "L0_gnn_a2", "L0_gnn_gamma", "L0_gnn_beta"]
_OUT = ((N, D), "float32")


def kernel(**inputs):
    import numpy as _np
    import concourse.bacc as _bacc
    from concourse import mybir as _mybir
    from concourse.bass_utils import run_bass_kernel_spmd as _run

    nc = _bacc.Bacc("TRN2", target_bir_lowering=False, num_devices=1)
    arrays, args = {}, []
    for name in _INS:
        a = _np.ascontiguousarray(inputs[name])
        arrays[f"in_{name}"] = a
        args.append(nc.dram_tensor(f"in_{name}", a.shape, _mybir.dt.from_np(a.dtype), kind="ExternalInput").ap())
    shape, dtype = _OUT
    out = nc.dram_tensor("out", shape, _mybir.dt.from_np(_np.dtype(dtype)), kind="ExternalOutput").ap()
    gat_kernel(nc, *args, out)
    return _run(nc, [arrays], core_ids=[0]).results[0]["out"]
```

```python
from contextlib import ExitStack
from functools import partial

import concourse.bass as bass
from concourse import mybir

F32 = mybir.dt.float32
F32R = mybir.dt.float32r
BF16 = mybir.dt.bfloat16
I32 = mybir.dt.int32
U16 = mybir.dt.uint16
ALU = mybir.AluOpType
ACT = mybir.ActivationFunctionType
AX_X = mybir.AxisListType.X
RMAX = bass.bass_isa.ReduceOp.max

P = 128
N = 8192
D = 128
NB = N // P
SLOPE = 0.2
EPS = 1e-5
TINY = 1e-37

GB = 4
GI = GB * P
NG = N // GI
PAIR = 2
STEPS = NB // PAIR
CS = 4
CJ = CS * PAIR * P
BUFS = 4
BODY = CS * BUFS
BODIES = STEPS // BODY
SLOTS = 4
LOOK = SLOTS + 1
DC = D + 2
TW = DC + D
DB = D + 1
TWO = 2
TWOS = 2
LEAD = 4
CONV = 80
LAG = 2
SPLIT = 200
XB = 8
XG = NB // XB
PER_BANK = 3
BANKS = (XB + PER_BANK - 1) // PER_BANK
PIECE = NB // 4


def gat_kernel(nc, x, adj, w, a1, a2, gamma, beta, out):
    ctx = ExitStack()
    with ctx:
        def sb(name, shape, dt=F32):
            return ctx.enter_context(nc.sbuf_tensor(name, shape, dt))

        def sem(name):
            return ctx.enter_context(nc.semaphore(name))

        adj_sb = sb("adj_sb", [P, BUFS, GB * CJ], I32)
        adj_bf = sb("adj_bf", [P, TWOS, GB, TWO * PAIR * P], BF16)
        table = sb("table", [P, NB, TW], F32R)
        table_b = sb("table_b", [P, NB, DB], BF16)
        p_rows = sb("p_rows", [P, 2, GI])
        wgt = sb("wgt", [P, SLOTS, PAIR * GI])
        wgt_h = sb("wgt_h", [P, SLOTS, PAIR * GI], F32R)
        wgt_l = sb("wgt_l", [P, SLOTS, PAIR * GI], BF16)
        sums = sb("sums", [P, GB, TW])
        work = sb("work", [P, GB, D])
        x_res = sb("x_res", [P, GB, D])
        ident_bf = sb("ident_bf", [P, P], BF16)
        a_sb = sb("a_sb", [P, 2])
        gamma_sb = sb("gamma_sb", [P, D])
        beta_sb = sb("beta_sb", [P, D])
        top = sb("top", [P, 2])
        q_cols = sb("q_cols", [P, NB])
        g_cols = sb("g_cols", [P, NB])
        den = sb("den", [P, GB])
        rden = sb("rden", [P, GB])
        stats = sb("stats", [P, GB, 6])
        mean_sum = sb("mean_sum", [P, GB])
        mean_gap = sb("mean_gap", [P, GB])
        sq_sum = sb("sq_sum", [P, GB])
        var_eps = sb("var_eps", [P, GB])
        neg_mean = sb("neg_mean", [P, GB])
        rstd = sb("rstd", [P, GB])
        minus_half = sb("minus_half", [P, GB])

        at_ps = ctx.enter_context(nc.psum_tensor("at_ps", [P, SLOTS, 512], F32))
        acc = ctx.enter_context(nc.psum_tensor("acc", [P, GB, 512], F32))
        p_dram = nc.dram_tensor("p_dram", [NB, P], F32, kind="Internal").ap()

        agg = sums[:, :, 0:D]
        spare = sums[:, :, :].rearrange("p b k -> p (b k)")
        w_sb, ident, p_t = spare[:, 0:D], spare[:, D:2 * D], spare[0:NB, 2 * D:2 * D + P]
        wt = spare[:, 3 * D:3 * D + DC]
        s_cols = spare[:, 4 * D + 2:4 * D + 2 + 2 * NB].rearrange("p (b o) -> p b o", o=2)
        gap = spare[:, 5 * D + 2:5 * D + 2 + NB]
        rise = spare[:, 5 * D + 2 + NB:5 * D + 2 + 2 * NB]
        p_cols = spare[:, 6 * D + 2:6 * D + 2 + NB]
        x_st = [wgt[:, u, :].rearrange("p (b k) -> p b k", b=XB) for u in range(2)]
        xt_sb = [wgt[:, 2 + u, :] for u in range(2)]
        xt_ps = [at_ps[:, 2 * u:2 * u + 2, :].rearrange("p a k -> p (a k)") for u in range(2)]
        misc = acc[:, BANKS, :]
        wh = adj_sb[:, 2:4, :].bitcast(F32).rearrange("p a (b k) -> p (a b) k", k=D)
        qh_all, ql_all = table[:, :, 0:D], table[:, :, DC:DC + D]

        w_loaded = sem("w_loaded")
        affine_loaded = sem("affine_loaded")
        x_loaded = [sem(f"x_loaded{u}") for u in range(2)]
        x_turned = sem("x_turned")
        xt_ready = sem("xt_ready")
        wh_ps = sem("wh_ps")
        wh_ready = sem("wh_ready")
        ident_zero = sem("ident_zero")
        consts_ready = sem("consts_ready")
        wt_ps = sem("wt_ps")
        wt_ready = sem("wt_ready")
        top_part = sem("top_part")
        top_ready = sem("top_ready")
        gap_ready = sem("gap_ready")
        factors_ready = sem("factors_ready")
        p_turned = sem("p_turned")
        p_t_ready = sem("p_t_ready")
        p_stored = sem("p_stored")
        p_loaded = sem("p_loaded")
        scaled = sem("scaled")
        qh_ready = sem("qh_ready")
        table_dve = sem("table_dve")
        table_pool = sem("table_pool")
        adj_loaded = [sem(f"adj_loaded{k}") for k in range(BUFS)]
        conv_act = sem("conv_act")
        conv_dve = sem("conv_dve")
        at_ready = sem("at_ready")
        e_ready = sem("e_ready")
        eh_ready = sem("eh_ready")
        el_dve = sem("el_dve")
        el_pool = sem("el_pool")
        used = sem("used")
        bank_done = sem("bank_done")
        acc_free = sem("acc_free")
        numer_ready = sem("numer_ready")
        den_ready = sem("den_ready")
        rden_ready = sem("rden_ready")
        agg_ready = sem("agg_ready")
        neg_ready = sem("neg_ready")
        elu_ready = sem("elu_ready")
        elu_sum = sem("elu_sum")
        x_res_loaded = sem("x_res_loaded")
        y_ready = sem("y_ready")
        stats_ready = sem("stats_ready")
        pair_ready = sem("pair_ready")
        moment_ready = sem("moment_ready")
        var_ready = sem("var_ready")
        rstd_ready = sem("rstd_ready")
        centred = sem("centred")
        out_ready = sem("out_ready")
        out_stored = sem("out_stored")

        def xacc_of(b):
            c = (b % PER_BANK) * DC
            return acc[:, b // PER_BANK, c:c + DC]

        def blocks_in(bank):
            return min(PER_BANK, XB - bank * PER_BANK)

        def rows_of(t, first, blocks):
            return t[bass.ds(first * P, blocks * P), :].rearrange("(b p) k -> p b k", p=P)

        def ahead_of(s):
            a = s + LEAD
            return (a // CS) % BUFS, a % CS, a // BODY

        def slots_of(a):
            return adj_bf[:, (a // TWO) % TWOS, :, :]

        def columns(buf, k):
            c = k * PAIR * P
            return adj_sb[:, buf, :].rearrange("p (b j) -> p b j", b=GB)[:, :, c:c + TWO * PAIR * P]

        block = ctx.enter_context(nc.Block())

        @block.sync
        def _(sp):
            def load_chunk(g, c, buf):
                src = adj[bass.ds(g * GI, GI), bass.ds(c * CJ, CJ)].rearrange("(b p) j -> p b j", p=P)
                sp.dma_start(adj_sb[:, buf, :].rearrange("p (b j) -> p b j", b=GB), src).then_inc(adj_loaded[buf], 16)

            def load_quad(g, quad):
                for k in range(BUFS):
                    sp.wait_ge(conv_act, g * (STEPS // TWO) + (quad * BUFS + k - BUFS + 1) * (CS // TWO))
                    sp.wait_ge(conv_dve, g * (STEPS // TWO) + (quad * BUFS + k - BUFS + 1) * (CS // TWO))
                    load_chunk(g, quad * BUFS + k, k)

            def load_p(g):
                row = p_dram[bass.ds(g * GB, GB), :].rearrange("(o b) p -> o (b p)", o=1)
                sp.dma_start(p_rows[:, bass.ds(g % 2, 1), :],
                             row.broadcast_to([P, GI])).then_inc(p_loaded, 16)

            def load_x(g):
                sp.wait_ge(y_ready, g * 2)
                sp.dma_start(x_res[:, :, :], rows_of(x, g * GB, GB)).then_inc(x_res_loaded, 16)

            def store(g):
                sp.wait_ge(out_ready, g * GB + GB)
                sp.dma_start(rows_of(out, g * GB, GB), work[:, :, :]).then_inc(out_stored, 16)

            sp.dma_start(w_sb[:, :], w).then_inc(w_loaded, 16)
            sp.dma_start(a_sb[:, 0:1], a1.rearrange("(k o) -> k o", o=1)).then_inc(w_loaded, 16)
            sp.dma_start(a_sb[:, 1:2], a2.rearrange("(k o) -> k o", o=1)).then_inc(w_loaded, 16)
            for u in range(2):
                sp.dma_start(x_st[u], rows_of(x, u * XB, XB)).then_inc(x_loaded[u], 16)
            with sp.Fori(1, XG // 2) as n:
                for u in range(2):
                    sp.wait_ge(x_turned, n * 2 + (u - 1))
                    sp.dma_start(x_st[u], rows_of(x, (n * 2 + u) * XB, XB)).then_inc(x_loaded[u], 16)
            sp.dma_start(gamma_sb[:, :], gamma.partition_broadcast(P)).then_inc(affine_loaded, 16)
            sp.dma_start(beta_sb[:, :], beta.partition_broadcast(P)).then_inc(affine_loaded, 16)
            load_chunk(0, 0, 0)
            load_chunk(0, 1, 1)
            sp.wait_ge(p_t_ready, 1)
            sp.dma_start(p_dram, p_t[:, :]).then_inc(p_stored, 16)
            sp.wait_ge(p_stored, 16)
            load_p(0)
            sp.wait_ge(table_dve, 5)
            sp.wait_ge(table_pool, 2)
            load_chunk(0, 2, 2)
            load_chunk(0, 3, 3)

            load_quad(0, 1)
            load_p(1)
            load_quad(1, 0)
            load_x(0)
            with sp.Fori(1, NG - 1) as g:
                load_quad(g, 1)
                sp.wait_ge(e_ready, g * STEPS)
                load_p(g + 1)
                load_quad(g + 1, 0)
                load_x(g)
                store(g - 1)
            load_quad(NG - 1, 1)
            load_x(NG - 1)
            store(NG - 2)
            store(NG - 1)
            sp.wait_ge(out_stored, 16 * NG + 16)

        @block.tensor
        def _(pe):
            def turn_tiles(a):
                tile = at_ps[:, a % SLOTS, :].bitcast(BF16)
                for k in range(PAIR):
                    for b in range(GB):
                        c = (k * GB + b) * P
                        j = (a % TWO * PAIR + k) * P
                        mm = nc.tensor.transpose(tile[:, c:c + P], slots_of(a)[:, b, j:j + P], ident_bf[:, :])
                mm.then_inc(at_ready, 1)

            def multiply(g, body, s):
                step, j, slot = g * STEPS + body * BODY + s, (body * BODY + s) * PAIR, s % SLOTS
                opens, closes = j == 0, j == NB - PAIR
                rows = [table[:, j + k, :] for k in range(PAIR)]
                pe.wait_ge(eh_ready, step + 1)
                for b in range(GB):
                    if opens:
                        pe.wait_ge(acc_free, g * GB + (b + 1))
                    for k in range(PAIR):
                        c = k * GI + b * P
                        nc.tensor.matmul(acc[:, b, 0:TW], wgt_h[:, slot, c:c + P], rows[k],
                                         start=opens and k == 0, stop=False, skip_group_check=True)
                pe.wait_ge(el_dve, step + (SLOTS + 1))
                pe.wait_ge(el_pool, step + (SLOTS + 1))
                for b in range(GB):
                    for k in range(PAIR):
                        c = k * GI + b * P
                        mm = nc.tensor.matmul(acc[:, b, 0:DB], wgt_l[:, slot, c:c + P], table_b[:, j + k, :],
                                              start=False, stop=closes and k == PAIR - 1, skip_group_check=True)
                    if closes and b < GB - 1:
                        mm.then_inc(bank_done, 1)
                mm.then_inc(used, 1)

            def turn_ahead(g, body, s):
                a = s + LOOK
                if a % TWO == 0:
                    twos = g * (STEPS // TWO) + body * (BODY // TWO)
                    pe.wait_ge(conv_act, twos + (a // TWO + 1))
                    pe.wait_ge(conv_dve, twos + (a // TWO + 1))
                pe.wait_ge(e_ready, g * STEPS + body * BODY + (a - SLOTS + 1))
                turn_tiles(a)

            def body_steps(g, body, ahead=BODY):
                for s in range(BODY):
                    multiply(g, body, s)
                    if s < ahead:
                        turn_ahead(g, body, s)

            pe.wait_ge(consts_ready, 3)
            pe.wait_ge(w_loaded, 16 * 3)
            nc.tensor.transpose(misc[:, 0:D], w_sb[:, :], ident[:, :])
            nc.tensor.matmul(misc[:, D:DC], w_sb[:, :], a_sb[:, :], start=True, stop=True).then_inc(wt_ps, 1)
            pe.wait_ge(wt_ready, 1)

            def turn_x(m, u, pair, first):
                pe.wait_ge(x_loaded[u], pair * 16 + 16)
                if not first:
                    pe.wait_ge(xt_ready, m - 1)
                for b in range(XB):
                    mm = nc.tensor.transpose(xt_ps[u][:, b * P:(b + 1) * P], x_st[u][:, b, :], ident[:, :])
                mm.then_inc(x_turned, 1)

            def project(m, u, first):
                pe.wait_ge(xt_ready, m + 1)
                if not first:
                    pe.wait_ge(wh_ready, m)
                for b in range(XB):
                    mm = nc.tensor.matmul(xacc_of(b), xt_sb[u][:, b * P:(b + 1) * P], wt[:, :], start=True, stop=True)
                mm.then_inc(wh_ps, 1)

            turn_x(0, 0, 0, True)
            turn_x(1, 1, 0, True)
            project(0, 0, True)
            project(1, 1, False)
            with pe.Fori(1, XG // 2) as n:
                turn_x(n * 2, 0, n, False)
                turn_x(n * 2 + 1, 1, n, False)
                project(n * 2, 0, False)
                project(n * 2 + 1, 1, False)

            pe.wait_ge(factors_ready, 3)
            nc.tensor.transpose(misc[0:NB, 0:P], p_cols[:, :], ident[:, :]).then_inc(p_turned, 1)

            for step in range(LOOK):
                if step == 0:
                    pe.wait_ge(xt_ready, XG)
                pe.wait_ge(conv_act, step // TWO + 1)
                pe.wait_ge(conv_dve, step // TWO + 1)
                if step >= SLOTS:
                    pe.wait_ge(e_ready, step - SLOTS + 1)
                turn_tiles(step)
            pe.wait_ge(table_dve, 5)
            pe.wait_ge(table_pool, 2)
            pe.wait_ge(wh_ready, XG)
            pe.wait_ge(p_t_ready, 1)
            with pe.Fori(0, NG - 1) as g:
                for body in range(BODIES):
                    body_steps(g, body)
            body_steps(NG - 1, 0)
            body_steps(NG - 1, BODIES - 1, BODY - LOOK)

        @block.scalar
        def _(act):
            def convert(step, buf, k, a):
                if step is not None:
                    act.wait_ge(at_ready, step + (TWO - TWOS * TWO))
                nc.scalar.copy(slots_of(a)[:, :, CONV:TWO * PAIR * P],
                               columns(buf, k)[:, :, CONV:TWO * PAIR * P]).then_inc(conv_act, 1)

            def convert_ahead(g, body, s):
                buf, k, use = ahead_of(s)
                if k == 0:
                    act.wait_ge(adj_loaded[buf], (g * BODIES + body) * 16 + (1 + use) * 16)
                convert(g * STEPS + body * BODY + (s + LEAD), buf, k, s + LEAD)

            def convert_first():
                for a in range(0, LEAD, TWO):
                    if a % CS == 0:
                        act.wait_ge(adj_loaded[a // CS], 16)
                    convert(None if a < TWOS * TWO else a, a // CS, a % CS, a)

            def high_part(step, slot):
                act.wait_ge(e_ready, step + 1)
                act.wait_ge(used, step + 1)
                nc.scalar.copy(wgt_h[:, slot, :], wgt[:, slot, :]).then_inc(eh_ready, 1)

            def take_sums(g):
                for b in range(GB):
                    if b < GB - 1:
                        act.wait_ge(bank_done, g * (GB - 1) + (b + 1))
                    else:
                        act.wait_ge(used, g * STEPS + (STEPS + SLOTS))
                    nc.scalar.copy(sums[:, b, :], acc[:, b, 0:TW]).then_inc(acc_free, 1)

            def divide(g, b):
                act.wait_ge(rden_ready, g + 1)
                act.wait_ge(numer_ready, g * 2 + (b // 2 + 1))
                nc.scalar.activation(agg[:, b, :], agg[:, b, :], ACT.Copy, scale=rden[:, b:b + 1]).then_inc(agg_ready, 1)

            def negative(g):
                act.wait_ge(agg_ready, g * GB + GB)
                act.wait_ge(out_stored, g * 16 + 16)
                nc.scalar.activation(work[:, :, :], agg[:, :, :], ACT.Relu, scale=-1.0).then_inc(neg_ready, 1)

            def exponential(g):
                act.wait_ge(neg_ready, g + 1)
                nc.scalar.activation(work[:, :, :], work[:, :, :], ACT.Exp, scale=-1.0).then_inc(elu_ready, 1)

            finals = {1: [take_sums], 12: [negative], 14: [exponential]}
            for b in range(GB):
                finals[5 + b + b // 2] = [partial(divide, b=b)]

            act.wait_ge(wt_ps, 1)
            nc.scalar.copy(wt[:, :], misc[:, 0:DC]).then_inc(wt_ready, 1)

            def copy_xt(m, u, first):
                act.wait_ge(x_turned, m + 1)
                if not first:
                    act.wait_ge(wh_ps, m - 1)
                nc.scalar.copy(xt_sb[u], xt_ps[u]).then_inc(xt_ready, 1)

            copy_xt(0, 0, True)
            copy_xt(1, 1, True)
            with act.Fori(1, XG // 2) as n:
                for u in range(2):
                    copy_xt(n * 2 + u, u, False)

            act.wait_ge(gap_ready, 2)
            nc.scalar.activation(p_cols[:, :], rise[:, :], ACT.Exp, scale=SLOPE - 1.0).then_inc(factors_ready, 1)
            nc.scalar.activation(q_cols[:, :], gap[:, :], ACT.Exp, scale=SLOPE).then_inc(factors_ready, 1)
            nc.scalar.activation(g_cols[:, :], gap[:, :], ACT.Exp, scale=1.0 - SLOPE).then_inc(factors_ready, 1)
            act.wait_ge(factors_ready, 2)
            nc.scalar.copy(table[:, :, D:D + 1], q_cols[:, :].rearrange("p (b o) -> p b o", o=1)).then_inc(qh_ready, 1)
            act.wait_ge(p_turned, 1)
            nc.scalar.copy(p_t[:, :], misc[0:NB, 0:P]).then_inc(p_t_ready, 1)
            for n in range(NB // PIECE):
                act.wait_ge(scaled, n + 1)
                nc.scalar.copy(qh_all[:, n * PIECE:(n + 1) * PIECE, :],
                               wh[:, n * PIECE:(n + 1) * PIECE, :]).then_inc(qh_ready, 1)

            def steps(g, body, last=None, ahead=BODY):
                for s in range(BODY):
                    if (s + LEAD) % TWO == 0 and s < ahead:
                        convert_ahead(g, body, s)
                    high_part(g * STEPS + body * BODY + s, s % SLOTS)
                    if last is not None:
                        for final in finals.get(body * BODY + s, []):
                            final(last)

            convert_first()
            with act.Fori(0, BODIES) as body:
                steps(0, body)
            with act.Fori(1, NG - 1) as g:
                for body in range(BODIES):
                    steps(g, body, g - 1)
            steps(NG - 1, 0, NG - 2)
            steps(NG - 1, BODIES - 1, NG - 2, ahead=BODY - LEAD)
            for s in sorted(finals):
                for final in finals[s]:
                    final(NG - 1)

        @block.vector
        def _(dve):
            def convert(step, buf, k, a):
                if step is not None:
                    dve.wait_ge(at_ready, step + (TWO - TWOS * TWO))
                nc.vector.tensor_copy(slots_of(a)[:, :, 0:CONV], columns(buf, k)[:, :, 0:CONV]).then_inc(conv_dve, 1)

            def convert_ahead(g, body, s):
                buf, k, use = ahead_of(s)
                if k == 0:
                    dve.wait_ge(adj_loaded[buf], (g * BODIES + body) * 16 + (1 + use) * 16)
                convert(g * STEPS + body * BODY + (s + LEAD), buf, k, s + LEAD)

            def convert_first():
                for a in range(0, LEAD, TWO):
                    if a % CS == 0:
                        dve.wait_ge(adj_loaded[a // CS], 16)
                    convert(None if a < TWOS * TWO else a, a // CS, a % CS, a)

            def weights(g, step, j, slot):
                dve.wait_ge(at_ready, step + 1)
                dve.wait_ge(el_dve, step + 1)
                dve.wait_ge(el_pool, step + 1)
                for k in range(PAIR):
                    ins = nc.vector.scalar_tensor_tensor(
                        out=wgt[:, slot, k * GI:(k + 1) * GI],
                        in0=p_rows[:, bass.ds(g % 2, 1), :].rearrange("p o i -> p (o i)"),
                        scalar=g_cols[:, bass.ds(j + k, 1)],
                        in1=at_ps[:, slot, :].bitcast(U16)[:, k * GI:(k + 1) * GI],
                        op0=ALU.max, op1=ALU.min)
                ins.then_inc(e_ready, 1)

            def low_part(step, slot):
                dve.wait_ge(eh_ready, step + 1)
                nc.vector.tensor_tensor(wgt_l[:, slot, 0:SPLIT], wgt[:, slot, 0:SPLIT],
                                        wgt_h[:, slot, 0:SPLIT].bitcast(F32), ALU.subtract).then_inc(el_dve, 1)

            def invert(g):
                dve.wait_ge(acc_free, g * GB + 2 * GB)
                nc.vector.scalar_tensor_tensor(out=den[:, :], in0=sums[:, :, D:D + 1].rearrange("p b o -> p (b o)"),
                                               scalar=TINY, in1=sums[:, :, D + 1:DC].rearrange("p b o -> p (b o)"),
                                               op0=ALU.max, op1=ALU.add).then_inc(den_ready, 1)
                dve.wait_ge(den_ready, g + 1)
                nc.vector.reciprocal(rden[:, :], den[:, :]).then_inc(rden_ready, 1)

            def numerator(g, two):
                nc.vector.tensor_tensor(agg[:, two, :], agg[:, two, :], sums[:, two, DC:TW],
                                        ALU.add).then_inc(numer_ready, 1)

            def join_elu(g, two):
                dve.wait_ge(elu_ready, g + 1)
                nc.vector.scalar_tensor_tensor(out=agg[:, two, :], in0=agg[:, two, :], scalar=0.0, in1=work[:, two, :],
                                               op0=ALU.max, op1=ALU.add).then_inc(elu_sum, 1)

            def residual(g, two):
                dve.wait_ge(elu_sum, g * 2 + (two.stop // 2))
                dve.wait_ge(x_res_loaded, g * 16 + 16)
                nc.vector.scalar_tensor_tensor(out=agg[:, two, :], in0=agg[:, two, :], scalar=-1.0, in1=x_res[:, two, :],
                                               op0=ALU.add, op1=ALU.add).then_inc(y_ready, 1)

            def statistics(g, b):
                dve.wait_ge(y_ready, g * 2 + (b // 2 + 1))
                nc.vector.bn_stats(stats[:, b, :], agg[:, b, :]).then_inc(stats_ready, 1)

            def moments(g):
                def stat(k):
                    return stats[:, :, k:k + 1].rearrange("p b o -> p (b o)")

                dve.wait_ge(stats_ready, g * GB + GB)
                nc.vector.tensor_tensor(mean_sum[:, :], stat(1), stat(4), ALU.add).then_inc(pair_ready, 1)
                nc.vector.tensor_tensor(mean_gap[:, :], stat(1), stat(4), ALU.subtract).then_inc(pair_ready, 1)
                nc.vector.tensor_tensor(sq_sum[:, :], stat(2), stat(5), ALU.add).then_inc(pair_ready, 1)

            def moments_end(g):
                dve.wait_ge(pair_ready, g * 3 + 3)
                nc.vector.tensor_scalar(neg_mean[:, :], mean_sum[:, :], -0.5, None, ALU.mult).then_inc(moment_ready, 1)
                nc.vector.tensor_scalar(sq_sum[:, :], sq_sum[:, :], 1.0 / D, EPS, ALU.mult,
                                        ALU.add).then_inc(moment_ready, 1)
                nc.vector.tensor_tensor(mean_gap[:, :], mean_gap[:, :], mean_gap[:, :],
                                        ALU.mult).then_inc(moment_ready, 1)
                dve.wait_ge(moment_ready, g * 3 + 3)
                nc.vector.scalar_tensor_tensor(out=var_eps[:, :], in0=mean_gap[:, :], scalar=0.25, in1=sq_sum[:, :],
                                               op0=ALU.mult, op1=ALU.add).then_inc(var_ready, 1)

            def centre(g, b):
                dve.wait_ge(moment_ready, g * 3 + 3)
                nc.vector.scalar_tensor_tensor(out=work[:, b, :], in0=agg[:, b, :], scalar=neg_mean[:, b:b + 1],
                                               in1=gamma_sb[:, :], op0=ALU.add, op1=ALU.mult).then_inc(centred, 1)

            def scale(g, b):
                dve.wait_ge(centred, g * GB + (b + 1))
                dve.wait_ge(rstd_ready, g + 1)
                nc.vector.scalar_tensor_tensor(out=work[:, b, :], in0=work[:, b, :], scalar=rstd[:, b:b + 1],
                                               in1=beta_sb[:, :], op0=ALU.mult, op1=ALU.add).then_inc(out_ready, 1)

            finals = {s: [] for s in range(STEPS)}
            finals[3].append(invert)
            for h in range(2):
                two = slice(h * 2, h * 2 + 2)
                finals[4 + h].append(partial(numerator, two=two))
                finals[17 + h * 2].append(partial(join_elu, two=two))
                finals[18 + h * 2].append(partial(residual, two=two))
            for b in range(GB):
                finals[19 + b].append(partial(statistics, b=b))
                finals[24 + b].append(partial(centre, b=b))
                finals[28 + b].append(partial(scale, b=b))
            finals[22].append(moments)
            finals[23].append(moments_end)

            def take_wh(m):
                dve.wait_ge(wh_ps, m + 1)
                for r in range(BANKS):
                    k = blocks_in(r)
                    src = acc[:, r, 0:k * DC].rearrange("p (b k) -> p b k", k=DC)
                    nc.vector.tensor_copy(wh[:, bass.ds(m * XB + r * PER_BANK, k), :], src[:, :, 0:D])
                    last = nc.vector.tensor_copy(s_cols[:, bass.ds(m * XB + r * PER_BANK, k), :], src[:, :, D:DC])
                last.then_inc(wh_ready, 1)

            with dve.Fori(0, XG) as m:
                take_wh(m)

            dve.wait_ge(wh_ready, XG)
            s_j = s_cols[:, :, 1:2].rearrange("p b o -> p (b o)")
            s_i = s_cols[:, :, 0:1].rearrange("p b o -> p (b o)")
            nc.vector.reduce_max(top[:, 0:1], s_j, AX_X).then_inc(top_part, 1)
            dve.wait_ge(top_ready, 1)
            nc.vector.tensor_scalar(rise[:, :], s_i, top[:, 1:2], 0.0, ALU.add, ALU.max).then_inc(gap_ready, 1)
            nc.vector.tensor_scalar(gap[:, :], s_j, top[:, 1:2], None, ALU.subtract).then_inc(gap_ready, 1)

            dve.wait_ge(factors_ready, 2)
            for n in range(NB // PIECE):
                lo, hi = n * PIECE, (n + 1) * PIECE
                q_wide = q_cols[:, lo:hi].rearrange("p (b o) -> p b o", o=1).broadcast_to([P, PIECE, D])
                nc.vector.tensor_tensor(wh[:, lo:hi, :], wh[:, lo:hi, :], q_wide, ALU.mult).then_inc(scaled, 1)
            dve.wait_ge(qh_ready, 1)
            nc.vector.tensor_tensor(table[:, :, D + 1:DC], q_cols[:, :].rearrange("p (b o) -> p b o", o=1),
                                    table[:, :, D:D + 1].bitcast(F32), ALU.subtract).then_inc(table_dve, 1)
            nc.vector.tensor_copy(table_b[:, :, D:DB],
                                  q_cols[:, :].rearrange("p (b o) -> p b o", o=1)).then_inc(table_dve, 1)
            dve.wait_ge(scaled, NB // PIECE)
            nc.vector.tensor_copy(table_b[:, :, 0:D], wh).then_inc(table_dve, 1)
            for n in range(2):
                dve.wait_ge(qh_ready, n + 2)
                nc.vector.tensor_tensor(ql_all[:, n * PIECE:(n + 1) * PIECE, :], wh[:, n * PIECE:(n + 1) * PIECE, :],
                                        qh_all[:, n * PIECE:(n + 1) * PIECE, :].bitcast(F32),
                                        ALU.subtract).then_inc(table_dve, 1)

            def steps(g, body, last=None, ahead=BODY, span=range(BODY), low=True):
                for s in span:
                    step = g * STEPS + body * BODY + s
                    if last is not None and body == 0 and s == 0:
                        dve.wait_ge(p_loaded, g * 16 + 16)
                    if (s + LEAD) % TWO == 0 and s < ahead:
                        convert_ahead(g, body, s)
                    weights(g, step, (body * BODY + s) * PAIR, s % SLOTS)
                    if low:
                        low_part(step - LAG, (s - LAG) % SLOTS)
                    if last is not None:
                        for final in finals.get(body * BODY + s, []):
                            final(last)

            convert_first()
            dve.wait_ge(affine_loaded, 16 * 2)
            dve.wait_ge(factors_ready, 3)
            dve.wait_ge(p_loaded, 16)
            steps(0, 0, span=range(LAG), low=False)
            steps(0, 0, span=range(LAG, BODY))
            with dve.Fori(1, BODIES) as body:
                steps(0, body)
            with dve.Fori(1, NG - 1) as g:
                for body in range(BODIES):
                    steps(g, body, last=g - 1)
            steps(NG - 1, 0, last=NG - 2)
            steps(NG - 1, BODIES - 1, last=NG - 2, ahead=BODY - LEAD)
            for k in range(LAG, 0, -1):
                low_part(NG * STEPS - k, (NG * STEPS - k) % SLOTS)
            for s in sorted(finals):
                for final in finals[s]:
                    final(NG - 1)

        @block.gpsimd
        def _(pool):
            def low_part(step, slot):
                pool.wait_ge(eh_ready, step + 1)
                nc.gpsimd.tensor_tensor(wgt_l[:, slot, SPLIT:PAIR * GI], wgt[:, slot, SPLIT:PAIR * GI],
                                        wgt_h[:, slot, SPLIT:PAIR * GI].bitcast(F32), ALU.subtract).then_inc(el_pool, 1)

            def deviation(g):
                pool.wait_ge(var_ready, g + 1)
                nc.gpsimd.tensor_tensor(rstd[:, :], var_eps[:, :], minus_half[:, :], ALU.pow).then_inc(rstd_ready, 1)

            finals = {24: [deviation]}

            nc.gpsimd.memset(ident[:, :], 0.0).then_inc(ident_zero, 1)
            pool.wait_ge(ident_zero, 1)
            nc.gpsimd.affine_select(out=ident[:, :], in_=ident[:, :], compare_op=ALU.not_equal, fill=1.0, base=0,
                                    pattern=[[-1, P]], channel_multiplier=1).then_inc(consts_ready, 1)
            pool.wait_ge(consts_ready, 1)
            nc.gpsimd.tensor_copy(ident_bf[:, :], ident[:, :]).then_inc(consts_ready, 1)
            nc.gpsimd.memset(minus_half[:, :], -0.5).then_inc(consts_ready, 1)
            pool.sem_inc(el_dve, SLOTS)
            pool.sem_inc(el_pool, SLOTS)
            pool.sem_inc(used, SLOTS)
            pool.sem_inc(acc_free, GB)
            pool.sem_inc(out_stored, 16)
            pool.wait_ge(top_part, 1)
            nc.gpsimd.partition_all_reduce(top[:, 1:2], top[:, 0:1], P, RMAX).then_inc(top_ready, 1)
            for n in range(2, 4):
                pool.wait_ge(qh_ready, n + 2)
                nc.gpsimd.tensor_tensor(ql_all[:, n * PIECE:(n + 1) * PIECE, :], wh[:, n * PIECE:(n + 1) * PIECE, :],
                                        qh_all[:, n * PIECE:(n + 1) * PIECE, :].bitcast(F32),
                                        ALU.subtract).then_inc(table_pool, 1)

            def steps(g, body, last=None):
                for s in range(BODY):
                    low_part(g * STEPS + body * BODY + s, s % SLOTS)
                    if last is not None:
                        for final in finals.get(body * BODY + s, []):
                            final(last)

            with pool.Fori(0, BODIES) as body:
                steps(0, body)
            with pool.Fori(1, NG) as g:
                for body in range(BODIES):
                    steps(g, body, last=g - 1)
            for s in sorted(finals):
                for final in finals[s]:
                    final(NG - 1)


_INS = ["x", "adj", "L0_gnn_W_w", "L0_gnn_a1", "L0_gnn_a2", "L0_gnn_gamma", "L0_gnn_beta"]
_OUT = ((N, D), "float32")


def kernel(**inputs):
    import numpy as _np
    import concourse.bacc as _bacc
    from concourse import mybir as _mybir
    from concourse.bass_utils import run_bass_kernel_spmd as _run

    nc = _bacc.Bacc("TRN2", target_bir_lowering=False, num_devices=1)
    arrays, args = {}, []
    for name in _INS:
        a = _np.ascontiguousarray(inputs[name])
        arrays[f"in_{name}"] = a
        args.append(nc.dram_tensor(f"in_{name}", a.shape, _mybir.dt.from_np(a.dtype), kind="ExternalInput").ap())
    shape, dtype = _OUT
    out = nc.dram_tensor("out", shape, _mybir.dt.from_np(_np.dtype(dtype)), kind="ExternalOutput").ap()
    gat_kernel(nc, *args, out)
    return _run(nc, [arrays], core_ids=[0]).results[0]["out"]
```
